# Optimizing a Trainium2 kernel written in Bass

```python
import numpy as np
import jax
import jax.numpy as jnp

def _softmax(x, axis=-1):
    return jax.nn.softmax(x, axis=axis)

def _gelu(x):
    return jax.nn.gelu(x, approximate=True)

def _silu(x):
    return jax.nn.silu(x)

def _sigmoid(x):
    return jax.nn.sigmoid(x)

def _layernorm(x, axis=-1, eps=1e-05):
    m = jnp.mean(x, axis=axis, keepdims=True)
    v = jnp.var(x, axis=axis, keepdims=True)
    return (x - m) / jnp.sqrt(v + eps)

def _scatter_add(tgt, idx, src, axis=0):
    return tgt.at[idx].add(src)

def _segment_sum(src, seg, n):
    return jax.ops.segment_sum(src, seg, n)
kernel_name = 'mk_seq_preln_d2_jaxref_r8_3bcebc'

def setup_inputs(seed: int=0):
    np.random.seed(seed)
    _w = jnp.asarray

    def _L0_attn_setup():
        import jax, jax.numpy as jnp
        import numpy as np
        D_MODEL = 256
        N_HEADS = 32
        N_KV_HEADS = 8
        HEAD_DIM = D_MODEL // N_HEADS
        N_REP = N_HEADS // N_KV_HEADS
        SCALE = HEAD_DIM ** (-0.5)

        def _rope_tables(seq_len):
            inv_freq = 1.0 / 10000.0 ** (jnp.arange(0, HEAD_DIM, 2, dtype=jnp.float32) / HEAD_DIM)
            t = jnp.arange(seq_len, dtype=jnp.float32)
            freqs = jnp.outer(t, inv_freq)
            return (jnp.cos(freqs), jnp.sin(freqs))

        def _apply_rope(x, cos, sin):
            x_r, x_i = (x[..., ::2], x[..., 1::2])
            out_r = x_r * cos - x_i * sin
            out_i = x_r * sin + x_i * cos
            out = jnp.stack([out_r, out_i], axis=-1)
            return out.reshape(x.shape)
        key = jax.random.key(seed)
        ks = jax.random.split(key, 5)
        bs, seq_len = (2, 256)
        std = D_MODEL ** (-0.5)
        x = jax.random.normal(ks[0], (bs, seq_len, D_MODEL), dtype=jnp.float32)
        wq = jax.random.normal(ks[1], (N_HEADS * HEAD_DIM, D_MODEL), dtype=jnp.float32) * std
        wk = jax.random.normal(ks[2], (N_KV_HEADS * HEAD_DIM, D_MODEL), dtype=jnp.float32) * std
        wv = jax.random.normal(ks[3], (N_KV_HEADS * HEAD_DIM, D_MODEL), dtype=jnp.float32) * std
        wo = jax.random.normal(ks[4], (D_MODEL, N_HEADS * HEAD_DIM), dtype=jnp.float32) * std
        return {'x': x, 'wq': wq, 'wk': wk, 'wv': wv, 'wo': wo}
    _L0_attn_in = _L0_attn_setup()

    def _L0_ffn_setup():
        import jax, jax.numpy as jnp
        import numpy as np
        HIDDEN = 256
        INTER = 128
        N_EXPERTS = 8
        TOP_K = 2

        def _swiglu(x, wg, wu, wd):
            return jax.nn.silu(x @ wg) * (x @ wu) @ wd
        key = jax.random.key(seed)
        ks = jax.random.split(key, 9)
        s = 0.02
        x = jax.random.normal(ks[0], (4, 256, HIDDEN), dtype=jnp.float32)
        Wr = jax.random.normal(ks[1], (N_EXPERTS, HIDDEN), dtype=jnp.float32) * s
        Wg = jax.random.normal(ks[2], (N_EXPERTS, HIDDEN, INTER), dtype=jnp.float32) * s
        Wu = jax.random.normal(ks[3], (N_EXPERTS, HIDDEN, INTER), dtype=jnp.float32) * s
        Wd = jax.random.normal(ks[4], (N_EXPERTS, INTER, HIDDEN), dtype=jnp.float32) * s
        Wg_s = jax.random.normal(ks[5], (HIDDEN, INTER), dtype=jnp.float32) * s
        Wu_s = jax.random.normal(ks[6], (HIDDEN, INTER), dtype=jnp.float32) * s
        Wd_s = jax.random.normal(ks[7], (INTER, HIDDEN), dtype=jnp.float32) * s
        return {'hidden_states': x, 'Wr': Wr, 'Wg': Wg, 'Wu': Wu, 'Wd': Wd, 'Wg_s': Wg_s, 'Wu_s': Wu_s, 'Wd_s': Wd_s}
    _L0_ffn_in = _L0_ffn_setup()

    def _L1_attn_setup():
        import jax, jax.numpy as jnp
        import numpy as np
        H = 16
        HKV = 4
        DK = 128
        DV = 128
        HID = 256
        KSZ = 4
        EPS = 1e-05
        NORMALIZER = 16.0

        def _causal_dwconv_silu(x, w):
            B, S, C = x.shape
            K = w.shape[1]
            xp = jnp.pad(x, ((0, 0), (K - 1, 0), (0, 0)))
            y = jnp.zeros_like(x)
            for i in range(K):
                y = y + w[:, i] * xp[:, i:i + S, :]
            return jax.nn.silu(y)

        def _l2norm(x, eps=1e-06):
            return x * jax.lax.rsqrt(jnp.sum(x * x, axis=-1, keepdims=True) + eps)
        key = jax.random.key(seed)
        ks = jax.random.split(key, 8)
        B, S = (2, 256)
        qkv_dim = H * DK + HKV * DK + HKV * DV
        s = lambda fan_in: 1.0 / np.sqrt(fan_in)
        return {'hidden_states': jax.random.normal(ks[0], (B, S, HID), jnp.float32), 'qkv_w': jax.random.uniform(ks[1], (qkv_dim, HID), jnp.float32, -s(HID), s(HID)), 'g_w': jax.random.uniform(ks[2], (H * DV, HID), jnp.float32, -s(HID), s(HID)), 'b_w': jax.random.uniform(ks[3], (H, HID), jnp.float32, -s(HID), s(HID)), 'gk_w': jax.random.uniform(ks[4], (H, HID), jnp.float32, -s(HID), s(HID)), 'conv_w': jax.random.uniform(ks[5], (qkv_dim, KSZ), jnp.float32, -s(KSZ), s(KSZ)), 'out_norm_w': jnp.ones((DV,), jnp.float32), 'o_w': jax.random.uniform(ks[6], (HID, H * DV), jnp.float32, -s(H * DV), s(H * DV))}
    _L1_attn_in = _L1_attn_setup()

    def _L1_ffn_setup():
        import jax, jax.numpy as jnp
        import numpy as np
        HIDDEN = 256
        INTER = 688
        LUT_SIZE = 16

        def _ghost_linear(x, idx, lut):
            w = lut[idx]
            return jnp.einsum('bsh,oh->bso', x, w)
        key = jax.random.key(seed)
        k_x, k_lut, k_g, k_u, k_d = jax.random.split(key, 5)
        x = jax.random.normal(k_x, (2, 512, HIDDEN), dtype=jnp.float32)
        lut = jax.random.normal(k_lut, (LUT_SIZE,), dtype=jnp.float32) * 0.02
        gate_idx = jax.random.randint(k_g, (INTER, HIDDEN), 0, LUT_SIZE, dtype=jnp.int32)
        up_idx = jax.random.randint(k_u, (INTER, HIDDEN), 0, LUT_SIZE, dtype=jnp.int32)
        down_idx = jax.random.randint(k_d, (HIDDEN, INTER), 0, LUT_SIZE, dtype=jnp.int32)
        return {'x': x, 'lut': lut, 'gate_idx': gate_idx, 'up_idx': up_idx, 'down_idx': down_idx}
    _L1_ffn_in = _L1_ffn_setup()
    _d = {'L0_attn_x': _L0_attn_in['x'], 'L0_attn_wq': _L0_attn_in['wq'], 'L0_attn_wk': _L0_attn_in['wk'], 'L0_attn_wv': _L0_attn_in['wv'], 'L0_attn_wo': _L0_attn_in['wo'], 'L0_ffn_Wr': _L0_ffn_in['Wr'], 'L0_ffn_Wg': _L0_ffn_in['Wg'], 'L0_ffn_Wu': _L0_ffn_in['Wu'], 'L0_ffn_Wd': _L0_ffn_in['Wd'], 'L0_ffn_Wg_s': _L0_ffn_in['Wg_s'], 'L0_ffn_Wu_s': _L0_ffn_in['Wu_s'], 'L0_ffn_Wd_s': _L0_ffn_in['Wd_s'], 'L1_attn_qkv_w': _L1_attn_in['qkv_w'], 'L1_attn_g_w': _L1_attn_in['g_w'], 'L1_attn_b_w': _L1_attn_in['b_w'], 'L1_attn_gk_w': _L1_attn_in['gk_w'], 'L1_attn_conv_w': _L1_attn_in['conv_w'], 'L1_attn_out_norm_w': _L1_attn_in['out_norm_w'], 'L1_attn_o_w': _L1_attn_in['o_w'], 'L1_ffn_lut': _L1_ffn_in['lut'], 'L1_ffn_gate_idx': _L1_ffn_in['gate_idx'], 'L1_ffn_up_idx': _L1_ffn_in['up_idx'], 'L1_ffn_down_idx': _L1_ffn_in['down_idx']}
    _x0 = _d['L0_attn_x']
    _d['L0_attn_x'] = jax.random.normal(jax.random.fold_in(jax.random.key(seed), 1), (16, 256, 256), dtype=_x0.dtype)
    del _x0
    return _d

def reference(L0_attn_x, L0_attn_wq, L0_attn_wk, L0_attn_wv, L0_attn_wo, L0_ffn_Wr, L0_ffn_Wg, L0_ffn_Wu, L0_ffn_Wd, L0_ffn_Wg_s, L0_ffn_Wu_s, L0_ffn_Wd_s, L1_attn_qkv_w, L1_attn_g_w, L1_attn_b_w, L1_attn_gk_w, L1_attn_conv_w, L1_attn_out_norm_w, L1_attn_o_w, L1_ffn_lut, L1_ffn_gate_idx, L1_ffn_up_idx, L1_ffn_down_idx):

    def _L0_attn_ref(x, wq, wk, wv, wo):
        import jax, jax.numpy as jnp
        import numpy as np
        D_MODEL = 256
        N_HEADS = 32
        N_KV_HEADS = 8
        HEAD_DIM = D_MODEL // N_HEADS
        N_REP = N_HEADS // N_KV_HEADS
        SCALE = HEAD_DIM ** (-0.5)

        def _rope_tables(seq_len):
            inv_freq = 1.0 / 10000.0 ** (jnp.arange(0, HEAD_DIM, 2, dtype=jnp.float32) / HEAD_DIM)
            t = jnp.arange(seq_len, dtype=jnp.float32)
            freqs = jnp.outer(t, inv_freq)
            return (jnp.cos(freqs), jnp.sin(freqs))

        def _apply_rope(x, cos, sin):
            x_r, x_i = (x[..., ::2], x[..., 1::2])
            out_r = x_r * cos - x_i * sin
            out_i = x_r * sin + x_i * cos
            out = jnp.stack([out_r, out_i], axis=-1)
            return out.reshape(x.shape)
        bs, seq_len, _ = x.shape
        q = (x @ wq.T).reshape(bs, seq_len, N_HEADS, HEAD_DIM).transpose(0, 2, 1, 3)
        k = (x @ wk.T).reshape(bs, seq_len, N_KV_HEADS, HEAD_DIM).transpose(0, 2, 1, 3)
        v = (x @ wv.T).reshape(bs, seq_len, N_KV_HEADS, HEAD_DIM).transpose(0, 2, 1, 3)
        cos, sin = _rope_tables(seq_len)
        q = _apply_rope(q, cos, sin)
        k = _apply_rope(k, cos, sin)
        k = jnp.repeat(k, N_REP, axis=1)
        v = jnp.repeat(v, N_REP, axis=1)
        attn = jnp.einsum('bhqd,bhkd->bhqk', q, k) * SCALE
        causal = jnp.triu(jnp.ones((seq_len, seq_len), dtype=bool), k=1)
        attn = jnp.where(causal, -jnp.inf, attn)
        attn = jax.nn.softmax(attn, axis=-1)
        out = jnp.einsum('bhqk,bhkd->bhqd', attn, v)
        out = out.transpose(0, 2, 1, 3).reshape(bs, seq_len, D_MODEL)
        return out @ wo.T

    def _L0_ffn_ref(hidden_states, Wr, Wg, Wu, Wd, Wg_s, Wu_s, Wd_s):
        import jax, jax.numpy as jnp
        import numpy as np
        HIDDEN = 256
        INTER = 128
        N_EXPERTS = 8
        TOP_K = 2

        def _swiglu(x, wg, wu, wd):
            return jax.nn.silu(x @ wg) * (x @ wu) @ wd
        B, S, H = hidden_states.shape
        flat = hidden_states.reshape(-1, H)
        T = flat.shape[0]
        shared_out = _swiglu(flat, Wg_s, Wu_s, Wd_s)
        logits = flat @ Wr.T
        topk_w, topk_idx = jax.lax.top_k(logits, TOP_K)
        topk_w = jax.nn.softmax(topk_w, axis=-1)
        combine = jnp.zeros((T, N_EXPERTS), dtype=flat.dtype)
        combine = combine.at[jnp.arange(T)[:, None], topk_idx].add(topk_w)
        routed_out = jnp.zeros_like(flat)
        for e in range(N_EXPERTS):
            routed_out = routed_out + combine[:, e:e + 1] * _swiglu(flat, Wg[e], Wu[e], Wd[e])
        return (shared_out + routed_out).reshape(B, S, H)

    def _L1_attn_ref(hidden_states, qkv_w, g_w, b_w, gk_w, conv_w, out_norm_w, o_w):
        import jax, jax.numpy as jnp
        import numpy as np
        H = 16
        HKV = 4
        DK = 128
        DV = 128
        HID = 256
        KSZ = 4
        EPS = 1e-05
        NORMALIZER = 16.0

        def _causal_dwconv_silu(x, w):
            B, S, C = x.shape
            K = w.shape[1]
            xp = jnp.pad(x, ((0, 0), (K - 1, 0), (0, 0)))
            y = jnp.zeros_like(x)
            for i in range(K):
                y = y + w[:, i] * xp[:, i:i + S, :]
            return jax.nn.silu(y)

        def _l2norm(x, eps=1e-06):
            return x * jax.lax.rsqrt(jnp.sum(x * x, axis=-1, keepdims=True) + eps)
        x = hidden_states
        B, S, _ = x.shape
        grp = H // HKV
        qkv = x @ qkv_w.T
        qkv = _causal_dwconv_silu(qkv, conv_w)
        q, k, v = jnp.split(qkv, [H * DK, H * DK + HKV * DK], axis=-1)
        q = q.reshape(B, S, H, DK)
        k = k.reshape(B, S, HKV, DK)
        v = v.reshape(B, S, HKV, DV)
        k = jnp.repeat(k, grp, axis=2)
        v = jnp.repeat(v, grp, axis=2)
        q = _l2norm(q) * DK ** (-0.5)
        k = _l2norm(k)
        g_log = jax.nn.log_sigmoid(x @ gk_w.T) / NORMALIZER
        alpha = jnp.exp(g_log)
        beta = jax.nn.sigmoid(x @ b_w.T)

        def step(Sstate, inp):
            q_t, k_t, v_t, a_t, b_t = inp
            Sstate = Sstate * a_t[..., None, None]
            v_pred = jnp.einsum('bhk,bhkv->bhv', k_t, Sstate)
            delta = (v_t - v_pred) * b_t[..., None]
            Sstate = Sstate + jnp.einsum('bhk,bhv->bhkv', k_t, delta)
            o_t = jnp.einsum('bhk,bhkv->bhv', q_t, Sstate)
            return (Sstate, o_t)
        tfirst = lambda a: jnp.moveaxis(a, 1, 0)
        S0 = jnp.zeros((B, H, DK, DV), x.dtype)
        _, o = jax.lax.scan(step, S0, (tfirst(q), tfirst(k), tfirst(v), tfirst(alpha), tfirst(beta)))
        o = jnp.moveaxis(o, 0, 1)
        g = (x @ g_w.T).reshape(B, S, H, DV)
        o = o * jax.lax.rsqrt(jnp.mean(o * o, axis=-1, keepdims=True) + EPS) * out_norm_w
        o = o * jax.nn.silu(g)
        return o.reshape(B, S, H * DV) @ o_w.T

    def _L1_ffn_ref(x, lut, gate_idx, up_idx, down_idx):
        import jax, jax.numpy as jnp
        import numpy as np
        HIDDEN = 256
        INTER = 688
        LUT_SIZE = 16

        def _ghost_linear(x, idx, lut):
            w = lut[idx]
            return jnp.einsum('bsh,oh->bso', x, w)
        gate = _ghost_linear(x, gate_idx, lut)
        up = _ghost_linear(x, up_idx, lut)
        h = jax.nn.silu(gate) * up
        return _ghost_linear(h, down_idx, lut)
    x = L0_attn_x
    x = x + _L0_attn_ref(_layernorm(x, axis=-1), L0_attn_wq, L0_attn_wk, L0_attn_wv, L0_attn_wo)
    x = x + _L0_ffn_ref(_layernorm(x, axis=-1), L0_ffn_Wr, L0_ffn_Wg, L0_ffn_Wu, L0_ffn_Wd, L0_ffn_Wg_s, L0_ffn_Wu_s, L0_ffn_Wd_s)
    x = x + _L1_attn_ref(_layernorm(x, axis=-1), L1_attn_qkv_w, L1_attn_g_w, L1_attn_b_w, L1_attn_gk_w, L1_attn_conv_w, L1_attn_out_norm_w, L1_attn_o_w)
    x = x + _L1_ffn_ref(_layernorm(x, axis=-1), L1_ffn_lut, L1_ffn_gate_idx, L1_ffn_up_idx, L1_ffn_down_idx)
    return x

_drawn_inputs = setup_inputs


def setup_inputs(seed=0):
    import zlib

    import numpy as np

    out = dict(_drawn_inputs(seed))
    spreads = {'L1_attn_out_norm_w': (1.0, 0.6)}
    factors = {'L0_ffn_Wr': 7.625,
     'L0_ffn_Wg': 6.735,
     'L0_ffn_Wu': 6.665,
     'L0_ffn_Wd': 6.678,
     'L0_ffn_Wg_s': 4.862,
     'L0_ffn_Wu_s': 4.753,
     'L0_ffn_Wd_s': 4.777,
     'L1_attn_gk_w': 56.936,
     'L1_attn_b_w': 7.663,
     'L1_ffn_lut': 5.813}
    for name, (base, spread) in spreads.items():
        noise = np.random.default_rng([zlib.crc32(name.encode()), seed]).standard_normal(out[name].shape)
        drawn = base * np.exp(spread * noise) if base else spread * noise
        out[name] = jnp.asarray(drawn.astype(out[name].dtype))
    for name, factor in factors.items():
        out[name] = (out[name] * factor).astype(out[name].dtype)
    return out
```

```python
from contextlib import ExitStack

import numpy as np

import concourse.bass as bass
from concourse import mybir
from concourse.alu_op_type import AluOpType as ALU

F32 = mybir.dt.float32
BF16 = mybir.dt.bfloat16
I32 = mybir.dt.int32
ACT = mybir.ActivationFunctionType
AX = mybir.AxisListType

P = 128
D = 256
KD = D // P
SEQ = 256
NT = SEQ // P
LN_EPS = 1e-5

NH, NKV, HD = 32, 8, 8
NQKV = NH * HD + 2 * NKV * HD
NROPE = NH * HD + NKV * HD
REP = NH // NKV
GROUPS = 4
HEAD_TILES = NH * HD // P
BIG = 1e30

NE, INTER = 8, 128

DH, DKV, DK = 16, 4, 128
DREP = DH // DKV
SUB = 32
NSUB = SEQ // SUB
QB = P // SUB
TAPS = 4
L2_EPS = 1e-6

FI = 688
FTILES = (FI + P - 1) // P
LUT = 16

BEFORE = 30000.0
WORK = 13300


class Arena:

    def __init__(self, tensor, size):
        self.tensor, self.size, self.at = tensor, size, 0

    def take(self, *dims):
        n = 1
        for d in dims:
            n *= d
        assert self.at + n <= self.size, (self.at + n, self.size)
        flat = self.tensor[:, self.at:self.at + n]
        self.at += n
        names = "abcd"[:len(dims)]
        if len(dims) == 1:
            return flat
        return flat.rearrange(f"p ({' '.join(names)}) -> p {' '.join(names)}",
                              **{k: d for k, d in zip(names, dims)})


def spread(ap, axis, n):
    new = ap.unsqueeze(axis)
    shape = list(new.shape)
    shape[axis] = n
    return new.to_broadcast(shape)


def load_weights(nc, dram, sb, C, lut_scratch):
    with ExitStack() as st:
        sem = lambda n: st.enter_context(nc.semaphore(n))
        loaded, zeroed = sem("weights_loaded"), sem("zeroed")
        idx_loaded = [sem("indices_loaded_even"), sem("indices_loaded_odd")]
        match, lut_sum, folded = sem("lut_match"), sem("lut_sum"), sem("norm_weight_folded")
        loads = C["loads"]
        chunks = C["lut_chunks"]
        with nc.Block() as block:
            @block.sync
            def _(sp):
                for dst, src in loads:
                    sp.dma_start(dst, src).then_inc(loaded, 16)
                for n, (rows, dst, src, width) in enumerate(chunks):
                    if n >= 2:
                        sp.wait_ge(lut_sum, LUT * (n - 1))
                    sp.dma_start(lut_scratch["idx"][n % 2][0:rows, 0:width], src).then_inc(idx_loaded[n % 2], 16)
                sp.wait_ge(loaded, 16 * len(loads))

            @block.gpsimd
            def _(pool):
                pool.memset(C["v32"], 0.0).then_inc(zeroed, 1)
                pool.memset(C["tri_inv"], 0.0).then_inc(zeroed, 1)
                pool.wait_ge(zeroed, 2)
                pool.memset(C["v32"][:, :, :, HD:HD + 1], 1.0).then_inc(zeroed, 1)
                pool.memset(C["tri_inv"][:, 0:SUB * SUB:SUB + 1], 1.0).then_inc(zeroed, 1)
                pool.memset(C["neg_half"], -0.5).then_inc(zeroed, 1)
                pool.memset(C["comb"], 1.0).then_inc(zeroed, 1)
                pool.memset(C["ones"], 1.0).then_inc(zeroed, 1)

            @block.vector
            def _(dve):
                dve.memset(C["bd"], 0.0)
                dve.wait_ge(loaded, 16 * len(loads))
                dve.tensor_copy(C["ident_bf"], C["ident"])
                dve.tensor_copy(C["before_bf"], C["before"])
                dve.tensor_scalar(C["o_w"], C["o_w"], C["norm_w"], None, ALU.mult).then_inc(folded, 1)
                for n, (rows, dst, src, width) in enumerate(chunks):
                    idx = lut_scratch["idx"][n % 2][0:rows, 0:width]
                    dve.wait_ge(idx_loaded[n % 2], 16 * (n // 2 + 1))
                    for v in range(LUT):
                        k = LUT * n + v
                        one = lut_scratch["term"][v % 2][0:rows, 0:width] if v else dst
                        if k >= 2:
                            dve.wait_ge(lut_sum, k - 1)
                        dve.tensor_scalar(one, idx, float(v), C["lut"][0:rows, v:v + 1],
                                          ALU.is_equal, ALU.mult).then_inc(match, 1)
                        dve.wait_ge(match, k + 1)
                        if v:
                            dve.wait_ge(lut_sum, k)
                            dve.tensor_tensor(dst, dst, one, ALU.add).then_inc(lut_sum, 1)
                        else:
                            dve.tensor_copy(dst, dst).then_inc(lut_sum, 1)
        nc.sync.sem_clear(C["all_sems"])
        nc.all_engine_barrier()


def norm_stats(dve, x, w, stats, aggr, var_ready):
    for t in range(NT):
        dve.bn_stats(w["bn6"][:, t, :], x[:, t, :]).then_inc(stats, 1)
    for t in range(NT):
        dve.wait_ge(stats, t + 1)
        dve.bn_aggr(w["mean_var"][:, t, :], w["bn6"][:, t, :]).then_inc(aggr, 1)
    dve.wait_ge(aggr, NT)
    dve.tensor_scalar(w["var_eps"], w["mean_var"][:, :, 1], LN_EPS, None, ALU.add).then_inc(var_ready, 1)


def norm_rstd(pool, C, w, var_ready, rstd_ready):
    pool.wait_ge(var_ready, 1)
    pool.tensor_tensor(w["rstd"], w["var_eps"], C["neg_half"][:, 0:NT], ALU.pow).then_inc(rstd_ready, 1)


def norm_apply(dve, x, w, rstd_ready, xn_ready):
    dve.wait_ge(rstd_ready, 1)
    for t in range(NT):
        dve.tensor_scalar(w["xn"][:, t, :], x[:, t, :], w["mean_var"][:, t, 0:1], w["rstd"][:, t:t + 1],
                          ALU.subtract, ALU.mult).then_inc(xn_ready, 1)


def norm_transpose(pe, C, w, bank, xn_ready, xnT_psum):
    for t in range(NT):
        pe.wait_ge(xn_ready, t + 1)
        for k in range(KD):
            mm = pe.transpose(bank[:, k * SEQ + t * P:k * SEQ + (t + 1) * P],
                              w["xn"][:, t, k * P:(k + 1) * P], C["ident"])
    mm.then_inc(xnT_psum, 1)


def norm_copy(act, w, bank, xnT_psum, xnT_ready):
    act.wait_ge(xnT_psum, 1)
    act.activation(w["xnT"].rearrange("p k n -> p (k n)"), bank[:], ACT.Copy).then_inc(xnT_ready, 1)


def norm_buffers(ar):
    return {"bn6": ar.take(NT, 6), "mean_var": ar.take(NT, 2), "var_eps": ar.take(NT), "rstd": ar.take(NT),
            "xn": ar.take(NT, D), "xnT": ar.take(KD, SEQ)}


def attention_layer(nc, C, ar, banks, x, x_in):
    ar.at = 0
    w = norm_buffers(ar)
    qk = ar.take(NT, NROPE)
    swapped = ar.take(NT, NROPE)
    k_rep = ar.take(NT, HEAD_TILES, P)
    qT = ar.take(HEAD_TILES, SEQ)
    probs = [ar.take(GROUPS, 3 * P) for _ in range(2)]
    probsT = ar.take(GROUPS, 3, P)
    neg_max = [ar.take(2 * GROUPS) for _ in range(2)]
    outT = ar.take(SEQ)
    inv_sum = ar.take(NT, GROUPS)
    heads_out = ar.take(NT, D)
    headsT = ar.take(KD, SEQ)
    v32, keys, mask = C["v32"], C["bd"], C["causal"]
    units = HEAD_TILES * REP
    scores = C["psum_scores"]

    def keys_of(u):
        return keys[:, u * GROUPS * SEQ:(u + 1) * GROUPS * SEQ]

    with ExitStack() as st:
        sem = lambda n: st.enter_context(nc.semaphore(n))
        x_loaded, stats, aggr, var_ready = sem("x_loaded"), sem("stats"), sem("aggr"), sem("var_ready")
        rstd_ready, xn_ready, xnT_psum, xnT_ready = sem("rstd_ready"), sem("xn_ready"), sem("xnT_psum"), sem("xnT_ready")
        qkv_mm, rope_cos, rope_sin, rope_done = sem("qkv_mm"), sem("rope_cos"), sem("rope_sin"), sem("rope_done")
        v_ready, krep_ready, qT_psum, qT_ready = sem("v_ready"), sem("krep_ready"), sem("qT_psum"), sem("qT_ready")
        kT_psum, keys_dve, keys_act = sem("kT_psum"), sem("keys_dve"), sem("keys_act")
        scores_mm, masked, exp_done = sem("scores_mm"), sem("masked"), sem("exp_done")
        probsT_mm, probsT_dve, probsT_act = sem("probsT_mm"), sem("probsT_dve"), sem("probsT_act")
        pv_mm, outT_ready, out_mm, recip_done, out_done = sem("pv_mm"), sem("outT_ready"), sem("out_mm"), sem("recip_done"), sem("out_done")
        headsT_mm, headsT_ready, wo_mm, x_done = sem("headsT_mm"), sem("headsT_ready"), sem("wo_mm"), sem("x_done")
        with nc.Block() as block:
            @block.sync
            def _(sp):
                sp.dma_start(x[:, :, :], x_in).then_inc(x_loaded, 16)

            @block.gpsimd
            def _(pool):
                norm_rstd(pool, C, w, var_ready, rstd_ready)

            @block.tensor
            def _(pe):
                norm_transpose(pe, C, w, banks[0], xn_ready, xnT_psum)
                pe.wait_ge(xnT_ready, 1)
                for t in range(NT):
                    for k in range(KD):
                        mm = pe.matmul(banks[1 + t][:, 0:NQKV], w["xnT"][:, k, t * P:(t + 1) * P], C["wqkv"][:, k, :],
                                       start=(k == 0), stop=(k == KD - 1))
                    mm.then_inc(qkv_mm, 1)
                for t in range(NT):
                    pe.wait_ge(rope_done, t + 1)
                    for i in range(HEAD_TILES):
                        mm = pe.transpose(banks[3][:, i * SEQ + t * P:i * SEQ + (t + 1) * P],
                                          qk[:, t, i * P:(i + 1) * P], C["ident"])
                mm.then_inc(qT_psum, 1)
                for t in range(NT):
                    pe.wait_ge(krep_ready, t + 1)
                    for i in range(HEAD_TILES):
                        mm = pe.transpose(banks[4 + i][:, t * P:(t + 1) * P], k_rep[:, t, i, :], C["ident"])
                mm.then_inc(kT_psum, 1)

                def score(u):
                    i, r = divmod(u, REP)
                    if i == 0:
                        pe.wait_ge(keys_dve, GROUPS * (r + 1))
                    else:
                        pe.wait_ge(keys_act, GROUPS * (r + 1))
                    if u:
                        pe.wait_ge(masked, 2 * GROUPS * u)
                    half = GROUPS * P
                    pe.matmul(scores[:, 0:half], qT[:, i, 0:P], keys_of(u)[:, 0:half], start=True, stop=True)
                    for m in range(2):
                        mm = pe.matmul(scores[:, (1 + m) * half:(2 + m) * half], qT[:, i, P:SEQ],
                                       keys_of(u)[:, m * half:(m + 1) * half], start=True, stop=True)
                    mm.then_inc(scores_mm, 1)

                def transpose_probs(u):
                    pe.wait_ge(exp_done, 2 * GROUPS * (u + 1))
                    if u == 0:
                        pe.wait_ge(keys_dve, GROUPS * REP)
                        pe.wait_ge(keys_act, GROUPS * REP)
                    else:
                        pe.wait_ge(probsT_dve, 2 * u)
                        pe.wait_ge(probsT_act, u)
                    for n in range(3 * GROUPS):
                        j, b = divmod(n, 3)
                        mm = pe.transpose(banks[3 + n // 4][:, n % 4 * P:(n % 4 + 1) * P],
                                          probs[u % 2][:, j, b * P:(b + 1) * P], C["ident"])
                        if n % 4 == 3:
                            mm.then_inc(probsT_mm, 1)

                def weigh_values(u):
                    i = u // REP
                    pe.wait_ge(probsT_dve, 2 * (u + 1))
                    pe.wait_ge(probsT_act, u + 1)
                    if u:
                        pe.wait_ge(outT_ready, u)
                    for j in range(GROUPS):
                        rows = slice(32 * j, 32 * j + 32)
                        pe.matmul(banks[6][rows, 0:SEQ], v32[:, 0, GROUPS * i + j, :],
                                  probsT[:, j, 0:2, :].rearrange("p b n -> p (b n)"), start=True, stop=False,
                                  skip_group_check=True)
                        mm = pe.matmul(banks[6][rows, P:SEQ], v32[:, 1, GROUPS * i + j, :],
                                       probsT[:, j, 2, :], start=False, stop=True, skip_group_check=True)
                    mm.then_inc(pv_mm, 1)

                def transpose_out(u):
                    pe.wait_ge(outT_ready, u + 1)
                    if u:
                        pe.wait_ge(out_done, u)
                    for t in range(NT):
                        mm = pe.transpose(banks[7][:, t * P:(t + 1) * P], outT[:, t * P:(t + 1) * P], C["ident"])
                    mm.then_inc(out_mm, 1)

                pe.wait_ge(qT_ready, 1)
                pe.wait_ge(v_ready, NT)
                score(0)
                for u in range(units):
                    if u + 1 < units:
                        score(u + 1)
                    transpose_probs(u)
                    if u:
                        transpose_out(u - 1)
                    weigh_values(u)
                transpose_out(units - 1)
                pe.wait_ge(out_done, units)
                for t in range(NT):
                    for k in range(KD):
                        mm = pe.transpose(banks[3][:, k * SEQ + t * P:k * SEQ + (t + 1) * P],
                                          heads_out[:, t, k * P:(k + 1) * P], C["ident"])
                mm.then_inc(headsT_mm, 1)
                pe.wait_ge(headsT_ready, 1)
                for t in range(NT):
                    for k in range(KD):
                        mm = pe.matmul(banks[4][:, t * D:(t + 1) * D], headsT[:, k, t * P:(t + 1) * P], C["wo"][:, k, :],
                                       start=(k == 0), stop=(k == KD - 1))
                mm.then_inc(wo_mm, 1)

            @block.scalar
            def _(act):
                norm_copy(act, w, banks[0], xnT_psum, xnT_ready)
                act.wait_ge(qT_psum, 1)
                act.activation(qT.rearrange("p i n -> p (i n)"), banks[3][:], ACT.Copy).then_inc(qT_ready, 1)
                act.wait_ge(kT_psum, 1)
                for r in range(REP):
                    for j in range(GROUPS):
                        rows = slice(32 * j, 32 * j + 32)
                        act.activation(keys_of(REP + r)[rows].rearrange("p (u j k) -> p u j k", j=GROUPS, k=32)[:, :, j, :],
                                       banks[5][rows, 0:SEQ].rearrange("p (u k) -> p u k", k=32), ACT.Copy,
                                       scale=C["repeat_rows"][rows, r:r + 1]).then_inc(keys_act, 1)

                def finish(u):
                    act.wait_ge(probsT_mm, 3 * (u + 1))
                    if u:
                        act.wait_ge(pv_mm, u)
                    act.activation(probsT.rearrange("p j b n -> p (j b n)")[:, 8 * P:12 * P], banks[5][:],
                                   ACT.Copy).then_inc(probsT_act, 1)
                    act.wait_ge(pv_mm, u + 1)
                    if u:
                        act.wait_ge(out_mm, u)
                    act.activation(outT, banks[6][:, 0:SEQ], ACT.Copy).then_inc(outT_ready, 1)

                for u in range(units + 1):
                    if u < units:
                        for n in range(2 * GROUPS):
                            b, j = divmod(n, GROUPS)
                            cols = probs[u % 2][:, j, P:3 * P] if b else probs[u % 2][:, j, 0:P]
                            act.wait_ge(masked, 2 * GROUPS * u + n + 1)
                            act.activation(cols, cols, ACT.Exp, bias=neg_max[u % 2][:, n:n + 1],
                                           scale=-1.0).then_inc(exp_done, 1)
                    if u:
                        finish(u - 1)
                act.wait_ge(headsT_mm, 1)
                act.activation(headsT.rearrange("p k n -> p (k n)"), banks[3][:], ACT.Copy).then_inc(headsT_ready, 1)

            @block.vector
            def _(dve):
                dve.wait_ge(x_loaded, 16)
                norm_stats(dve, x, w, stats, aggr, var_ready)
                norm_apply(dve, x, w, rstd_ready, xn_ready)
                for t in range(NT):
                    dve.wait_ge(qkv_mm, t + 1)
                    src = banks[1 + t]
                    pairs = src[:, 0:NROPE].rearrange("p (n c) -> p n c", c=2)
                    sin = C["rope_sin"][:, t, :].rearrange("p (n c) -> p n c", c=2)
                    out = swapped[:, t, :].rearrange("p (n c) -> p n c", c=2)
                    dve.tensor_tensor(qk[:, t, :], src[:, 0:NROPE], C["rope_cos"][:, t, :], ALU.mult).then_inc(rope_cos, 1)
                    for c in range(2):
                        dve.tensor_tensor(out[:, :, c], pairs[:, :, 1 - c], sin[:, :, c], ALU.mult).then_inc(rope_sin, 1)
                    dve.tensor_copy(v32[:, t, :, 0:HD],
                                    src[:, NROPE:NQKV].rearrange("p (g d) -> p g d", d=HD)).then_inc(v_ready, 1)
                for t in range(NT):
                    dve.wait_ge(rope_sin, 2 * NT)
                    dve.tensor_tensor(qk[:, t, :], qk[:, t, :], swapped[:, t, :], ALU.add).then_inc(rope_done, 1)
                for t in range(NT):
                    dve.wait_ge(rope_done, NT)
                    for i in range(HEAD_TILES):
                        k4 = qk[:, t, NH * HD + i * 32:NH * HD + i * 32 + 32].rearrange("p (g d) -> p g d", d=HD)
                        last = dve.tensor_copy(k_rep[:, t, i, :].rearrange("p (g r d) -> p g r d", r=REP, d=HD),
                                               spread(k4, 2, REP))
                    last.then_inc(krep_ready, 1)
                dve.wait_ge(kT_psum, 1)
                for r in range(REP):
                    for j in range(GROUPS):
                        rows = slice(32 * j, 32 * j + 32)
                        dve.tensor_scalar(keys_of(r)[rows].rearrange("p (u j k) -> p u j k", j=GROUPS, k=32)[:, :, j, :],
                                          banks[4][rows, 0:SEQ].rearrange("p (u k) -> p u k", k=32),
                                          C["repeat_rows"][rows, r:r + 1], None, ALU.mult).then_inc(keys_dve, 1)

                def mask_max(u):
                    dve.wait_ge(scores_mm, u + 1)
                    if u >= 2:
                        dve.wait_ge(probsT_mm, 3 * (u - 1))
                    for n in range(2 * GROUPS):
                        b, j = divmod(n, GROUPS)
                        if b:
                            src, m, dst = scores[:, GROUPS * P:], mask[:, :, :], probs[u % 2][:, j, P:3 * P]
                        else:
                            src, m, dst = scores[:, 0:GROUPS * P], mask[:, 4:8, :], probs[u % 2][:, j, 0:P]
                        src = src.rearrange("p (u j k) -> p u j k", j=GROUPS, k=32)[:, :, j, :]
                        dve.tensor_tensor_reduce(dst.rearrange("p (u k) -> p u k", k=32), src, m, 1.0, 3.0e38, ALU.add, ALU.min,
                                                 neg_max[u % 2][:, n:n + 1]).then_inc(masked, 1)

                def finish(u):
                    for m in range(2):
                        dve.wait_ge(probsT_mm, 3 * u + m + 1)
                        if u:
                            dve.wait_ge(pv_mm, u)
                        dve.tensor_copy(probsT.rearrange("p j b n -> p (j b n)")[:, m * 4 * P:(m + 1) * 4 * P],
                                        banks[3 + m][:]).then_inc(probsT_dve, 1)

                def normalise(u):
                    i, r = divmod(u, REP)
                    dve.wait_ge(out_mm, u + 1)
                    part = banks[7][:, 0:SEQ].rearrange("p (t j d) -> p t j d", t=NT, j=GROUPS)
                    dve.reciprocal(inv_sum, part[:, :, :, HD]).then_inc(recip_done, 1)
                    dve.wait_ge(recip_done, u + 1)
                    dst = heads_out.rearrange("p t (i j r d) -> p t i j r d", i=HEAD_TILES, j=GROUPS, r=REP)
                    dve.tensor_tensor(dst[:, :, i, :, r, :], part[:, :, :, 0:HD], spread(inv_sum, 3, HD),
                                      ALU.mult).then_inc(out_done, 1)

                for u in range(units + 2):
                    if u < units:
                        mask_max(u)
                    if 1 <= u <= units:
                        finish(u - 1)
                    if u >= 2:
                        normalise(u - 2)
                dve.wait_ge(wo_mm, 1)
                dve.tensor_tensor(x[:, :, :], x[:, :, :], banks[4][:].rearrange("p (t n) -> p t n", t=NT),
                                  ALU.add).then_inc(x_done, 1)
        nc.sync.sem_clear(C["all_sems"])
        nc.all_engine_barrier()


def experts_layer(nc, C, ar, banks, x):
    ar.at = 0
    w = norm_buffers(ar)
    logits, shifted, weight = ar.take(NT, NE), ar.take(NT, NE), ar.take(NT, NE)
    above, level = ar.take(NT, NE, NE), ar.take(NT, NE, NE)
    rank, chosen = ar.take(NT, NE), ar.take(NT, NE)
    top, total, inv_total = ar.take(NT), ar.take(NT), ar.take(NT)
    gate = [ar.take(SEQ) for _ in range(2)]
    hT = [ar.take(SEQ) for _ in range(2)]
    comb = C["comb"]
    order = [NE] + list(range(NE))
    n_exp = len(order)

    with ExitStack() as st:
        sem = lambda n: st.enter_context(nc.semaphore(n))
        stats, aggr, var_ready = sem("stats"), sem("aggr"), sem("var_ready")
        rstd_ready, xn_ready, xnT_psum, xnT_ready = sem("rstd_ready"), sem("xn_ready"), sem("xnT_psum"), sem("xnT_ready")
        router_mm, route, exp_ready, comb_ready = sem("router_mm"), sem("route"), sem("exp_ready"), sem("comb_ready")
        up_mm, gate_ready, hT_ready, down_mm, x_added = sem("up_mm"), sem("gate_ready"), sem("hT_ready"), sem("down_mm"), sem("x_added")
        shift_ready = sem("shift_ready")
        with nc.Block() as block:
            @block.gpsimd
            def _(pool):
                norm_rstd(pool, C, w, var_ready, rstd_ready)

            @block.tensor
            def _(pe):
                norm_transpose(pe, C, w, banks[0], xn_ready, xnT_psum)
                pe.wait_ge(xnT_ready, 1)
                for t in range(NT):
                    for k in range(KD):
                        mm = pe.matmul(banks[1][:, t * NE:(t + 1) * NE], w["xnT"][:, k, t * P:(t + 1) * P],
                                       C["router"][:, k, :], start=(k == 0), stop=(k == KD - 1))
                mm.then_inc(router_mm, 1)

                def up(n):
                    e = order[n]
                    if n >= 2:
                        pe.wait_ge(hT_ready, n - 1)
                    for half in range(2):
                        for k in range(KD):
                            mm = pe.matmul(banks[2 + n % 2][:, half * SEQ:(half + 1) * SEQ],
                                           C["gate_up"][:, k, e, half, :], w["xnT"][:, k, :],
                                           start=(k == 0), stop=(k == KD - 1))
                    mm.then_inc(up_mm, 1)

                def down(n):
                    pe.wait_ge(hT_ready, n + 1)
                    if n >= 2:
                        pe.wait_ge(x_added, NT * (n - 1))
                    for t in range(NT):
                        mm = pe.matmul(banks[4 + n % 2][:, t * D:(t + 1) * D], hT[n % 2][:, t * P:(t + 1) * P],
                                       C["down"][:, order[n], :], start=True, stop=True)
                    mm.then_inc(down_mm, 1)

                up(0)
                for n in range(n_exp):
                    if n + 1 < n_exp:
                        up(n + 1)
                    down(n)

            @block.scalar
            def _(act):
                norm_copy(act, w, banks[0], xnT_psum, xnT_ready)
                act.wait_ge(shift_ready, 1)
                act.activation(weight, shifted, ACT.Exp).then_inc(exp_ready, 1)
                for n in range(n_exp):
                    act.wait_ge(up_mm, n + 1)
                    if n >= 2:
                        act.wait_ge(hT_ready, n - 1)
                    act.activation(gate[n % 2], banks[2 + n % 2][:, 0:SEQ], ACT.Silu).then_inc(gate_ready, 1)

            @block.vector
            def _(dve):
                norm_stats(dve, x, w, stats, aggr, var_ready)
                norm_apply(dve, x, w, rstd_ready, xn_ready)
                dve.wait_ge(router_mm, 1)
                steps = [0]

                def step(ins):
                    steps[0] += 1
                    ins.then_inc(route, 1)
                    dve.wait_ge(route, steps[0])

                step(dve.tensor_copy(logits, banks[1][:, 0:NT * NE].rearrange("p (t e) -> p t e", t=NT)))
                dve.tensor_reduce(top, logits, AX.X, ALU.max).then_inc(route, 1)
                steps[0] += 1
                dve.wait_ge(route, steps[0])
                dve.tensor_tensor(shifted, logits, spread(top, 2, NE), ALU.subtract).then_inc(shift_ready, 1)
                mine, others = spread(logits, 3, NE), spread(logits, 2, NE)
                step(dve.tensor_tensor(above, others, mine, ALU.is_gt))
                step(dve.tensor_tensor(level, others, mine, ALU.is_equal))
                step(dve.tensor_tensor(level, level, spread(C["earlier"], 1, NT), ALU.mult))
                step(dve.tensor_tensor(above, above, level, ALU.add))
                step(dve.tensor_reduce(rank, above, AX.X, ALU.add))
                step(dve.tensor_scalar(chosen, rank, 1.5, None, ALU.is_lt))
                dve.wait_ge(exp_ready, 1)
                step(dve.tensor_tensor(weight, weight, chosen, ALU.mult))
                step(dve.tensor_reduce(total, weight, AX.X, ALU.add))
                step(dve.reciprocal(inv_total, total))
                dve.tensor_tensor(comb[:, :, 0:NE], weight, spread(inv_total, 2, NE), ALU.mult).then_inc(comb_ready, 1)
                for n in range(n_exp + 1):
                    if n < n_exp:
                        dve.wait_ge(gate_ready, n + 1)
                        if n >= 2:
                            dve.wait_ge(down_mm, n - 1)
                        dve.tensor_tensor(hT[n % 2], gate[n % 2], banks[2 + n % 2][:, SEQ:2 * SEQ],
                                          ALU.mult).then_inc(hT_ready, 1)
                    if n:
                        e = order[n - 1]
                        dve.wait_ge(down_mm, n)
                        dve.wait_ge(comb_ready, 1)
                        for t in range(NT):
                            dve.wait_ge(x_added, NT * (n - 1))
                            dve.scalar_tensor_tensor(x[:, t, :], banks[4 + (n - 1) % 2][:, t * D:(t + 1) * D],
                                                     comb[:, t, e:e + 1], x[:, t, :], ALU.mult, ALU.add).then_inc(x_added, 1)
        nc.sync.sem_clear(C["all_sems"])
        nc.all_engine_barrier()


def delta_layer(nc, C, ar, banks, x, dram):
    ar.at = 0
    w = {"bn6": ar.take(NT, 6), "mean_var": ar.take(NT, 2), "var_eps": ar.take(NT), "rstd": ar.take(NT),
         "xnT": ar.take(KD, SEQ)}
    kT, kn0 = ar.take(DKV, SEQ), ar.take(DKV, P)
    v_tok, kk = ar.take(NT, DKV, P), ar.take(NT, DKV, P)
    conv = [ar.take(2, SEQ) for _ in range(2)]
    bg = ar.take(NT, 2 * DH)
    neg_beta, decay, neg_gamma_beta = ar.take(NT, DH), ar.take(2, DH), ar.take(DH)
    sum_k, k_eps, rnorm_k, junk = ar.take(NT, DKV), ar.take(NT, DKV), ar.take(NT, DKV), ar.take(P)
    sys_beta, sys_g, sys_c = ar.take(SUB), ar.take(SUB), ar.take(SUB)
    sum_q, sum_o, rms_a, rms_b, rms = (ar.take(DREP) for _ in range(5))
    qT = [ar.take(DREP, SEQ) for _ in range(2)]
    k_raw, v_raw = qT
    slot_at = ar.at
    slots = [ar.take(DREP, P) for _ in range(11)]
    g_incl, gamma, probsT, bT, wt, t64, u64, u128, rhs, silu_g, state = slots
    delta, scaled, o_gated, o_gatedT = t64, u64, u128, probsT
    early = Arena(ar.tensor, ar.at)
    early.at = slot_at + 9 * DREP * P
    z, z_min, z_abs, e_abs, e_abs1 = (early.take(NT, 2 * DH) for _ in range(5))
    e_min, sig_den, log1 = early.take(NT, DH), early.take(NT, DH), early.take(NT, DH)
    w["xn"] = g_incl.rearrange("p a b -> p (a b)").rearrange("p (t n) -> p t n", t=NT)
    kn1 = gamma
    bgT = probsT.rearrange("p a b -> p (a b)")[:, 0:SEQ]
    kn = [kn0, kn1]
    square = lambda n: ar.tensor[:, slot_at + n * 512:slot_at + n * 512 + 1024]
    rows_cols = lambda ap: ap.rearrange("p (i j) -> p i j", j=SUB)
    sys_a, sys_d, sys_prod, sys_u = rows_cols(square(3)), rows_cols(square(5)), square(7), rows_cols(square(9))
    sys_t = rows_cols(C["tri_inv"])
    bd = C["bd"].rearrange("p (u q j) -> p u q j", q=QB, j=SUB)
    flat = lambda ap: ap.rearrange("p a b -> p (a b)")
    per_head = lambda ap: spread(ap, 2, P)
    bank4 = lambda bank: bank.rearrange("p (r n) -> p r n", r=DREP)
    t32 = lambda c, h: C["bd"][:, (c * DH + h) * P:(c * DH + h + 1) * P]
    u32 = lambda c, h: C["bd"][:, (DH * NT + c * DH + h) * P:(DH * NT + c * DH + h + 1) * P]
    t32s = lambda c, g: bank4(C["bd"][:, (c * DH + DREP * g) * P:(c * DH + DREP * (g + 1)) * P])
    u32s = lambda c, g: bank4(C["bd"][:, (DH * NT + c * DH + DREP * g) * P:(DH * NT + c * DH + DREP * (g + 1)) * P])
    units = [divmod(n, NT) for n in range(DKV * NT)]
    chunk = lambda c: slice(c * P, (c + 1) * P)

    tiles = [DH + n for n in range(2 * DKV)] + list(range(DH))
    step_tiles = [(tiles[2 * s], tiles[2 * s + 1]) for s in range(len(tiles) // 2)]
    q_step = lambda g, half: 4 + 2 * g + half

    def projected(s):
        if s < 2:
            return k_raw[:, 2 * s:2 * s + 2, :]
        if s < 4:
            return v_raw[:, 2 * s - 4:2 * s - 2, :]
        g, half = divmod(s - 4, 2)
        return qT[g % 2][:, 2 * half:2 * half + 2, :]

    with ExitStack() as st:
        sem = lambda n: st.enter_context(nc.semaphore(n))
        stats, aggr, var_ready = sem("stats"), sem("aggr"), sem("var_ready")
        rstd_ready, xn_ready, xnT_psum, xnT_ready = sem("rstd_ready"), sem("xn_ready"), sem("xnT_psum"), sem("xnT_ready")
        proj_mm, conv_first, conv_step, silu_done = sem("proj_mm"), sem("conv_first"), sem("conv_step"), sem("silu_done")
        z_mm, gate_step, e_ready, log_ready, bg_ready = sem("z_mm"), sem("gate_step"), sem("e_ready"), sem("log_ready"), sem("bg_ready")
        c_mm, bgT_mm, decay_ready, bgT_ready, ngb_ready = sem("c_mm"), sem("bgT_mm"), sem("decay_ready"), sem("bgT_ready"), sem("ngb_ready")
        k_tok_mm, sum_k_ready, k_eps_ready, rnorm_ready = sem("k_tok_mm"), sem("sum_k_ready"), sem("k_eps_ready"), sem("rnorm_ready")
        kn_ready, kT_mm, kT_ready, kk_mm, kk_ready = sem("kn_ready"), sem("kT_mm"), sem("kT_ready"), sem("kk_mm"), sem("kk_ready")
        v_tok_mm, v_ready = sem("v_tok_mm"), sem("v_ready")
        kk_stored, bg_stored, sys_bg_loaded, sys_kk_loaded = sem("kk_stored"), sem("bg_stored"), sem("sys_bg_loaded"), sem("sys_kk_loaded")
        sys_step, sys_exp, inv_step, inv_done = sem("sys_step"), sem("sys_exp"), sem("inv_step"), sem("inv_done")
        tu_stored, tu_loaded = sem("tu_stored"), sem("tu_loaded")
        g_ready, d_mm, gamma_ready, kq_mm, probs_ready, b_ready = (
            sem("g_ready"), sem("d_mm"), sem("gamma_ready"), sem("kq_mm"), sem("probs_ready"), sem("b_ready"))
        q_tok_mm, sum_q_ready, w_mm, w_ready = sem("q_tok_mm"), sem("sum_q_ready"), sem("w_mm"), sem("w_ready")
        t64_mm, t64_ready, u_mm, u_ready = sem("t64_mm"), sem("t64_ready"), sem("u_mm"), sem("u_ready")
        silu_mm, silu_g_ready, bv_ready, ks_mm, rhs_ready = sem("silu_mm"), sem("silu_g_ready"), sem("bv_ready"), sem("ks_mm"), sem("rhs_ready")
        delta_mm, delta_ready, decayed_ready, o_mm, qs_mm = sem("delta_mm"), sem("delta_ready"), sem("decayed_ready"), sem("o_mm"), sem("qs_mm")
        qs_ready, o_ready, sum_o_ready, rms_step, rms_ready = sem("qs_ready"), sem("o_ready"), sem("sum_o_ready"), sem("rms_step"), sem("rms_ready")
        gated_ready, gatedT_mm, gatedT_ready, y_mm, x_added = sem("gated_ready"), sem("gatedT_mm"), sem("gatedT_ready"), sem("y_mm"), sem("x_added")
        state_mm, state_ready = sem("state_mm"), sem("state_ready")
        n_tu = 2 * NT * QB

        with nc.Block() as block:
            @block.sync
            def _(sp):
                sp.wait_ge(bgT_ready, 1)
                sp.dma_start(dram["bg"], bgT[0:2 * DH, :]).then_inc(bg_stored, 16)
                sp.wait_ge(kk_ready, NT)
                for c in range(NT):
                    for q in range(QB):
                        rows = slice(SUB * q, SUB * q + SUB)
                        sp.dma_start(dram["kk"].rearrange("g b i j -> b i g j")[c * QB + q],
                                     kk[rows, c, :, rows]).then_inc(kk_stored, 16)
                sp.wait_ge(bg_stored, 16)
                sp.dma_start(sys_beta, dram["bg"][0:DH].rearrange("h (b i) -> (h b) i", i=SUB)).then_inc(sys_bg_loaded, 16)
                sp.dma_start(sys_g, dram["bg"][DH:2 * DH].rearrange("h (b i) -> (h b) i", i=SUB)).then_inc(sys_bg_loaded, 16)
                sp.wait_ge(kk_stored, 16 * NT * QB)
                for g in range(DKV):
                    for r in range(DREP):
                        at = (g * DREP + r) * NSUB
                        sp.dma_start(sys_a[at:at + NSUB], dram["kk"][g]).then_inc(sys_kk_loaded, 16)
                sp.wait_ge(inv_done, 1)
                sp.dma_start(dram["t"], sys_t).then_inc(tu_stored, 16)
                sp.wait_ge(inv_done, 2)
                sp.dma_start(dram["u"], sys_u).then_inc(tu_stored, 16)
                sp.wait_ge(tu_stored, 32)
                for m, name in enumerate("tu"):
                    src = dram[name].rearrange("(h c q) i j -> c q i h j", c=NT, q=QB)
                    for c in range(NT):
                        for q in range(QB):
                            u = (m * NT + c) * DH
                            sp.dma_start(bd[SUB * q:SUB * q + SUB, u:u + DH, q, :], src[c, q]).then_inc(tu_loaded, 16)

            @block.gpsimd
            def _(pool):
                norm_rstd(pool, C, w, var_ready, rstd_ready)
                pool.wait_ge(sum_k_ready, NT * DKV)
                pool.tensor_scalar(flat(k_eps), flat(sum_k), L2_EPS, None, ALU.add).then_inc(k_eps_ready, 1)
                pool.wait_ge(k_eps_ready, 1)
                pool.tensor_tensor(flat(rnorm_k), flat(k_eps), C["neg_half"], ALU.pow).then_inc(rnorm_ready, 1)

                def masked_decays(n):
                    g, c = units[n]
                    pool.wait_ge(bg_ready, 1)
                    pool.wait_ge(xnT_psum, 1)
                    if n:
                        pool.wait_ge(d_mm, n)
                    pool.tensor_tensor(g_incl, spread(C["incl"], 1, DREP),
                                       per_head(bg[:, c, DH + DREP * g:DH + DREP * (g + 1)]), ALU.mult).then_inc(g_ready, 1)

                masked_decays(0)
                pool.wait_ge(tu_stored, 32)
                for n, (g, c) in enumerate(units):
                    heads = slice(DREP * g, DREP * (g + 1))
                    pool.wait_ge(gamma_ready, n + 1)
                    pool.wait_ge(kk_ready, NT)
                    if n:
                        pool.wait_ge(w_mm, 2 * n)
                    pool.tensor_tensor(bT, spread(kk[:, c, g, :], 1, DREP), gamma, ALU.mult).then_inc(b_ready, 1)
                    if n:
                        pool.wait_ge(delta_mm, n)
                    pool.wait_ge(v_ready, NT)
                    pool.tensor_tensor(rhs, spread(v_tok[:, c, g, :], 1, DREP), per_head(bg[:, c, heads]),
                                       ALU.mult).then_inc(bv_ready, 1)
                    if n + 1 < len(units):
                        masked_decays(n + 1)
                    if c == 0:
                        pool.wait_ge(decay_ready, 1)
                        pool.wait_ge(delta_ready, n + 1)
                        pool.wait_ge(u_ready, 2 * n + 2)
                        pool.tensor_tensor(scaled, delta, per_head(decay[:, 1, heads]), ALU.mult).then_inc(decayed_ready, 1)
                    pool.wait_ge(rms_step, 2 * (n + 1))
                    pool.tensor_tensor(rms, rms_b, C["neg_half"][:, 0:DREP], ALU.pow).then_inc(rms_ready, 1)

            @block.tensor
            def _(pe):
                def project(s):
                    if s >= 3:
                        pe.wait_ge(conv_step, 6 * (s - 2))
                    for i, tile in enumerate(step_tiles[s]):
                        for k in range(KD):
                            mm = pe.matmul(banks[2 + s % 3][:, i * SEQ:(i + 1) * SEQ], C["qkv_w"][:, k, tile * P:(tile + 1) * P],
                                           w["xnT"][:, k, :], start=(k == 0), stop=(k == KD - 1))
                    mm.then_inc(proj_mm, 1)

                norm_transpose(pe, C, w, banks[0], xn_ready, xnT_psum)
                pe.wait_ge(xnT_ready, 1)
                for t in range(NT):
                    for k in range(KD):
                        mm = pe.matmul(banks[1][:, t * 2 * DH:(t + 1) * 2 * DH], w["xnT"][:, k, chunk(t)],
                                       C["bgk_w"][:, k, :], start=(k == 0), stop=(k == KD - 1))
                mm.then_inc(z_mm, 1)
                for s in range(3):
                    project(s)
                pe.wait_ge(bg_ready, 1)
                pe.matmul(banks[1][:, 64:64 + DH], C["incl"], bg[:, 1, DH:2 * DH], start=True, stop=True)
                pe.matmul(banks[1][:, 64 + DH:64 + 2 * DH], C["later"], bg[:, 0, DH:2 * DH],
                          start=True, stop=True).then_inc(c_mm, 1)
                for t in range(NT):
                    mm = pe.transpose(banks[7][0:2 * DH, chunk(t)], bg[:, t, :], C["ident"])
                mm.then_inc(bgT_mm, 1)
                pe.wait_ge(silu_done, 4)
                for c in range(NT):
                    for g in range(DKV):
                        mm = pe.transpose(banks[5 + c][:, g * P:(g + 1) * P], k_raw[:, g, chunk(c)], C["ident"])
                    mm.then_inc(k_tok_mm, 1)
                project(3)
                for c in range(NT):
                    pe.wait_ge(kn_ready, c + 1)
                    for g in range(DKV):
                        mm = pe.transpose(banks[5 + c][:, g * P:(g + 1) * P], kn[c][:, g, :], C["ident"])
                    mm.then_inc(kT_mm, 1)
                for c in range(NT):
                    pe.wait_ge(kT_ready, c + 1)
                    for g in range(DKV):
                        mm = pe.matmul(banks[5 + c][:, g * P:(g + 1) * P], kT[:, g, chunk(c)], kT[:, g, chunk(c)],
                                       start=True, stop=True)
                    mm.then_inc(kk_mm, 1)
                pe.wait_ge(silu_done, 8)
                pe.wait_ge(bgT_ready, 1)
                for c in range(NT):
                    for g in range(DKV):
                        mm = pe.transpose(banks[0 if c == 0 else 7][:, g * P:(g + 1) * P], v_raw[:, g, chunk(c)], C["ident"])
                    mm.then_inc(v_tok_mm, 1)
                project(q_step(0, 0))
                project(q_step(0, 1))

                for n, (g, c) in enumerate(units):
                    q = qT[g % 2]
                    pe.wait_ge(g_ready, n + 1)
                    if n:
                        pe.wait_ge(x_added, n)
                    else:
                        pe.wait_ge(v_ready, NT)
                    pe.matmul(banks[0], C["later"], flat(g_incl), start=True, stop=False)
                    pe.matmul(bank4(banks[0]), C["ident_bf"], spread(C["before_bf"], 1, DREP),
                              start=False, stop=True).then_inc(d_mm, 1)
                    pe.wait_ge(silu_done, 2 * (q_step(g, 1) + 1))
                    pe.wait_ge(kT_ready, NT)
                    if n:
                        pe.wait_ge(gatedT_ready, n)
                    else:
                        pe.wait_ge(decay_ready, 1)
                    pe.matmul(bank4(banks[1]), kT[:, g, chunk(c)], q[:, :, chunk(c)], start=True, stop=True).then_inc(kq_mm, 1)
                    if n:
                        pe.wait_ge(u_ready, 2 * n)
                    else:
                        pe.wait_ge(kk_ready, NT)
                    for r in range(DREP):
                        mm = pe.transpose(banks[5][:, r * P:(r + 1) * P], q[:, r, chunk(c)], C["ident"])
                    mm.then_inc(q_tok_mm, 1)

                    def joint(right, mm_sem):
                        for r in range(DREP):
                            mm = pe.matmul(banks[6][:, r * P:(r + 1) * P], bT[:, r, :], right(r), start=True, stop=True)
                        mm.then_inc(mm_sem, 1)

                    pe.wait_ge(b_ready, n + 1)
                    if n:
                        pe.wait_ge(o_ready, n)
                    else:
                        pe.wait_ge(tu_loaded, 16 * n_tu)
                    joint(lambda r: t32(c, DREP * g + r), w_mm)
                    if g + 1 < DKV:
                        project(q_step(g + 1, c))
                    pe.wait_ge(w_ready, 8 * n + 4)
                    if n:
                        pe.wait_ge(state_ready, (n + 1) // 2)
                        pe.wait_ge(silu_g_ready, n)
                    for r in range(DREP):
                        mm = pe.matmul(banks[7][:, r * P:(r + 1) * P], u32(c, DREP * g + r), wt[:, r, :], start=True, stop=True)
                    mm.then_inc(t64_mm, 1)
                    pe.wait_ge(sum_q_ready, DREP * (n + 1))
                    for r in range(DREP):
                        mm = pe.matmul(banks[5][:, r * P:(r + 1) * P], wt[:, r, :], u32(c, DREP * g + r), start=True, stop=True)
                    mm.then_inc(u_mm, 1)
                    pe.wait_ge(t64_ready, n + 1)
                    joint(lambda r: t64[:, r, :], w_mm)
                    for k in range(KD):
                        mm = pe.matmul(banks[7], w["xnT"][:, k, chunk(c)], C["g_w"][:, k, g * 512:(g + 1) * 512],
                                       start=(k == 0), stop=(k == KD - 1))
                    mm.then_inc(silu_mm, 1)
                    if c == 1:
                        pe.wait_ge(gamma_ready, n + 1)
                        pe.wait_ge(state_ready, g + 1)
                        pe.matmul(banks[0], kT[:, g, chunk(c)], flat(state), start=True, stop=True).then_inc(ks_mm, 1)
                    pe.wait_ge(w_ready, 8 * n + 8)
                    pe.wait_ge(u_ready, 2 * n + 1)
                    for r in range(DREP):
                        mm = pe.matmul(banks[5][:, r * P:(r + 1) * P], wt[:, r, :], u64[:, r, :], start=True, stop=True)
                    mm.then_inc(u_mm, 1)
                    if c == 1:
                        pe.wait_ge(rhs_ready, DREP * (g + 1))
                        for r in range(DREP):
                            mm = pe.matmul(banks[0][:, r * P:(r + 1) * P], q[:, r, chunk(c)], state[:, r, :], start=True, stop=True)
                        mm.then_inc(qs_mm, 1)
                    pe.wait_ge(u_ready, 2 * n + 2)
                    pe.wait_ge(bv_ready, n + 1)
                    pe.wait_ge(probs_ready, n + 1)
                    for r in range(DREP):
                        mm = pe.matmul(banks[1][:, r * P:(r + 1) * P], u128[:, r, :], rhs[:, r, :], start=True, stop=True)
                    mm.then_inc(delta_mm, 1)
                    pe.wait_ge(delta_ready, n + 1)
                    for r in range(DREP):
                        mm = pe.matmul(banks[6][:, r * P:(r + 1) * P], probsT[:, r, :], delta[:, r, :], start=True, stop=True)
                    mm.then_inc(o_mm, 1)
                    if c == 0:
                        pe.wait_ge(decayed_ready, g + 1)
                        pe.wait_ge(silu_g_ready, n + 1)
                        pe.matmul(banks[7], kn0[:, g, :], flat(scaled), start=True, stop=True).then_inc(state_mm, 1)
                    pe.wait_ge(gated_ready, DREP * (n + 1))
                    for r in range(DREP):
                        mm = pe.transpose(banks[1][:, r * P:(r + 1) * P], o_gated[:, r, :], C["ident"])
                    mm.then_inc(gatedT_mm, 1)
                    pe.wait_ge(gatedT_ready, n + 1)
                    if c == 1:
                        pe.wait_ge(qs_ready, DREP * (g + 1))
                    else:
                        pe.wait_ge(gamma_ready, n + 1)
                    for r in range(DREP):
                        mm = pe.matmul(banks[0][:, 0:D], o_gatedT[:, r, :], C["o_w"][:, DREP * g + r, :],
                                       start=(r == 0), stop=(r == DREP - 1))
                    mm.then_inc(y_mm, 1)

            @block.scalar
            def _(act):
                def conv_start(s):
                    act.wait_ge(proj_mm, s + 1)
                    if s >= 2:
                        act.wait_ge(silu_done, 2 * (s - 1))
                    for i, tile in enumerate(step_tiles[s]):
                        act.activation(conv[s % 2][:, i, :], banks[2 + s % 3][:, i * SEQ:(i + 1) * SEQ], ACT.Copy,
                                       scale=C["conv_w"][:, tile, TAPS - 1:TAPS]).then_inc(conv_first, 1)

                def conv_silu(s):
                    act.wait_ge(conv_step, 6 * (s + 1))
                    if s >= 8:
                        act.wait_ge(y_mm, 2 * ((s - 4) // 2 - 1))
                    elif s >= 4:
                        act.wait_ge(k_tok_mm, NT)
                        act.wait_ge(v_tok_mm, NT)
                    for i in range(2):
                        act.activation(projected(s)[:, i, :], conv[s % 2][:, i, :], ACT.Silu).then_inc(silu_done, 1)

                norm_copy(act, w, banks[0], xnT_psum, xnT_ready)
                for s in range(3):
                    conv_start(s)
                    if s:
                        conv_silu(s - 1)
                conv_silu(2)
                act.wait_ge(gate_step, 3)
                act.activation(e_abs, z_abs, ACT.Exp).then_inc(e_ready, 1)
                act.activation(e_min, z_min[:, :, 0:DH], ACT.Exp).then_inc(e_ready, 1)
                act.wait_ge(gate_step, 4)
                act.activation(log1, e_abs1[:, :, DH:2 * DH], ACT.Ln).then_inc(log_ready, 1)
                act.wait_ge(c_mm, 1)
                act.activation(flat(decay), banks[1][:, 64:64 + 2 * DH], ACT.Exp).then_inc(decay_ready, 1)
                for c in range(NT):
                    act.wait_ge(k_tok_mm, c + 1)
                    for g in range(DKV):
                        if c or g:
                            act.wait_ge(sum_k_ready, DKV * c + g)
                        act.activation(junk, banks[5 + c][:, g * P:(g + 1) * P], ACT.Square,
                                       accum_out=sum_k[:, c, g:g + 1]).then_inc(sum_k_ready, 1)
                conv_start(3)
                conv_silu(3)
                for c in range(NT):
                    act.wait_ge(kT_mm, c + 1)
                    act.activation(kT[:, :, chunk(c)], bank4(banks[5 + c]), ACT.Copy).then_inc(kT_ready, 1)
                for c in range(NT):
                    act.wait_ge(v_tok_mm, c + 1)
                    act.activation(flat(v_tok[:, c, :, :]), banks[0 if c == 0 else 7], ACT.Copy).then_inc(v_ready, 1)
                conv_start(q_step(0, 0))
                conv_start(q_step(0, 1))
                conv_silu(q_step(0, 0))
                conv_silu(q_step(0, 1))
                act.wait_ge(sys_step, 3)
                act.activation(sys_d, sys_d, ACT.Exp).then_inc(sys_exp, 1)

                for n, (g, c) in enumerate(units):
                    act.wait_ge(d_mm, n + 1)
                    if n:
                        act.wait_ge(probs_ready, n)
                        act.wait_ge(b_ready, n)
                    act.activation(flat(gamma), banks[0], ACT.Exp).then_inc(gamma_ready, 1)
                    act.wait_ge(q_tok_mm, n + 1)
                    if n:
                        act.wait_ge(rms_step, 2 * n)
                    for r in range(DREP):
                        if n or r:
                            act.wait_ge(sum_q_ready, DREP * n + r)
                        if n:
                            act.wait_ge(sum_o_ready, DREP * n)
                        act.activation(junk, banks[5][:, r * P:(r + 1) * P], ACT.Square,
                                       accum_out=sum_q[:, r:r + 1]).then_inc(sum_q_ready, 1)
                    if g + 1 < DKV:
                        conv_start(q_step(g + 1, c))
                    act.wait_ge(silu_mm, n + 1)
                    if n:
                        act.wait_ge(gated_ready, DREP * n)
                    act.activation(flat(silu_g), banks[7], ACT.Silu).then_inc(silu_g_ready, 1)
                    if g + 1 < DKV:
                        conv_silu(q_step(g + 1, c))
                    if c == 1:
                        act.wait_ge(qs_mm, g + 1)
                        act.wait_ge(u_ready, 2 * n + 2)
                        for r in range(DREP):
                            act.activation(scaled[:, r, :], banks[0][:, r * P:(r + 1) * P], ACT.Copy,
                                           scale=decay[:, 0, DREP * g + r:DREP * g + r + 1]).then_inc(qs_ready, 1)
                    act.wait_ge(delta_mm, n + 1)
                    act.activation(flat(delta), banks[1], ACT.Copy).then_inc(delta_ready, 1)
                    if c == 0:
                        act.wait_ge(state_mm, g + 1)
                        act.activation(flat(state), banks[7], ACT.Copy).then_inc(state_ready, 1)
                    act.wait_ge(o_ready, n + 1)
                    for r in range(DREP):
                        act.wait_ge(sum_q_ready, DREP * (n + 1))
                        if n or r:
                            act.wait_ge(sum_o_ready, DREP * n + r)
                        act.activation(junk, o_gated[:, r, :], ACT.Square, accum_out=sum_o[:, r:r + 1]).then_inc(sum_o_ready, 1)
                    act.wait_ge(gatedT_mm, n + 1)
                    act.activation(flat(o_gatedT), banks[1], ACT.Copy).then_inc(gatedT_ready, 1)

            @block.vector
            def _(dve):
                def convolve(s):
                    dve.wait_ge(conv_first, 2 * (s + 1))
                    for tap in range(TAPS - 1):
                        back = TAPS - 1 - tap
                        for i, tile in enumerate(step_tiles[s]):
                            if tap:
                                dve.wait_ge(conv_step, 6 * s + 2 * (tap - 1) + i + 1)
                            y = conv[s % 2][:, i, back:SEQ]
                            dve.scalar_tensor_tensor(y, banks[2 + s % 3][:, i * SEQ:(i + 1) * SEQ - back],
                                                     C["conv_w"][:, tile, tap:tap + 1], y, ALU.mult, ALU.add).then_inc(conv_step, 1)

                norm_stats(dve, x, w, stats, aggr, var_ready)
                norm_apply(dve, x, w, rstd_ready, xn_ready)
                dve.wait_ge(z_mm, 1)
                dve.tensor_copy(flat(z), banks[1][:, 0:NT * 2 * DH]).then_inc(gate_step, 1)
                dve.wait_ge(gate_step, 1)
                dve.tensor_scalar(z_min, z, 0.0, None, ALU.min).then_inc(gate_step, 1)
                dve.scalar_tensor_tensor(flat(z_abs), flat(z), -1.0, flat(z), ALU.mult, ALU.min).then_inc(gate_step, 1)
                convolve(0)
                convolve(1)
                convolve(2)
                dve.wait_ge(e_ready, 2)
                dve.tensor_scalar(e_abs1, e_abs, 1.0, None, ALU.add).then_inc(gate_step, 1)
                dve.wait_ge(gate_step, 4)
                dve.reciprocal(sig_den, e_abs1[:, :, 0:DH]).then_inc(gate_step, 1)
                dve.wait_ge(log_ready, 1)
                dve.tensor_tensor(log1, z_min[:, :, DH:2 * DH], log1, ALU.subtract).then_inc(gate_step, 1)
                dve.wait_ge(gate_step, 6)
                dve.tensor_tensor(bg[:, :, 0:DH], e_min, sig_den, ALU.mult).then_inc(gate_step, 1)
                dve.wait_ge(gate_step, 7)
                dve.tensor_scalar(neg_beta, bg[:, :, 0:DH], -1.0, None, ALU.mult).then_inc(gate_step, 1)
                dve.wait_ge(gate_step, 8)
                dve.tensor_scalar(bg[:, :, DH:2 * DH], log1, 1.0 / 16.0, None, ALU.mult).then_inc(bg_ready, 1)
                dve.wait_ge(bgT_mm, 1)
                dve.tensor_copy(bgT[0:2 * DH, :], banks[7][0:2 * DH, 0:SEQ]).then_inc(bgT_ready, 1)
                dve.wait_ge(decay_ready, 1)
                dve.tensor_tensor(neg_gamma_beta, neg_beta[:, 1, :], decay[:, 0, :], ALU.mult).then_inc(ngb_ready, 1)
                dve.wait_ge(rnorm_ready, 1)
                for c in range(NT):
                    dve.tensor_tensor(kn[c], bank4(banks[5 + c]), per_head(rnorm_k[:, c, :]), ALU.mult).then_inc(kn_ready, 1)
                convolve(3)
                for c in range(NT):
                    dve.wait_ge(kk_mm, c + 1)
                    dve.tensor_copy(flat(kk[:, c, :, :]), banks[5 + c]).then_inc(kk_ready, 1)
                convolve(q_step(0, 0))
                convolve(q_step(0, 1))
                dve.wait_ge(sys_bg_loaded, 32)
                dve.tensor_tensor_scan(sys_c, C["ones"], sys_g, 0.0, ALU.mult, ALU.add).then_inc(sys_step, 1)
                dve.wait_ge(sys_step, 1)
                dve.tensor_tensor(sys_d, spread(sys_c, 2, SUB), spread(sys_c, 1, SUB), ALU.subtract).then_inc(sys_step, 1)
                dve.wait_ge(sys_step, 2)
                dve.tensor_scalar(sys_d, sys_d, 0.0, None, ALU.min).then_inc(sys_step, 1)
                dve.wait_ge(sys_kk_loaded, 16 * DH)
                dve.wait_ge(sys_exp, 1)
                dve.tensor_tensor(sys_a, sys_a, sys_d, ALU.mult).then_inc(sys_step, 1)
                dve.wait_ge(sys_step, 4)
                dve.tensor_tensor(sys_a, sys_a, spread(sys_beta, 2, SUB), ALU.mult).then_inc(sys_step, 1)
                dve.wait_ge(sys_step, 5)
                for i in range(1, SUB):
                    prod = sys_prod[:, 0:i * i].rearrange("p (c j) -> p c j", j=i)
                    if i > 1:
                        dve.wait_ge(inv_step, 2 * (i - 1))
                    dve.tensor_tensor(prod, spread(sys_a[:, i, 0:i], 1, i), sys_t[:, 0:i, 0:i].rearrange("p j c -> p c j"),
                                      ALU.mult).then_inc(inv_step, 1)
                    dve.wait_ge(inv_step, 2 * i - 1)
                    last = dve.tensor_reduce(sys_t[:, i, 0:i], prod, AX.X, ALU.add, negate=True)
                    last.then_inc(inv_step if i < SUB - 1 else inv_done, 1)
                dve.wait_ge(inv_done, 1)
                dve.tensor_copy(sys_u, sys_t.rearrange("p i j -> p j i")).then_inc(inv_done, 1)
                dve.wait_ge(tu_stored, 32)

                for n, (g, c) in enumerate(units):
                    dve.wait_ge(kq_mm, n + 1)
                    dve.wait_ge(gamma_ready, n + 1)
                    if n:
                        dve.wait_ge(y_mm, n)
                    dve.tensor_tensor(probsT, bank4(banks[1]), gamma, ALU.mult).then_inc(probs_ready, 1)

                    def join_rows(mask):
                        for r in range(DREP):
                            dve.scalar_tensor_tensor(wt[:, r, :], banks[6][:, r * P:(r + 1) * P],
                                                     neg_beta[:, c, DREP * g + r:DREP * g + r + 1], mask,
                                                     ALU.mult, ALU.mult).then_inc(w_ready, 1)

                    dve.wait_ge(w_mm, 2 * n + 1)
                    if n:
                        dve.wait_ge(u_mm, 2 * n)
                    join_rows(C["cross64"])
                    dve.wait_ge(t64_mm, n + 1)
                    if n:
                        dve.wait_ge(o_mm, n)
                        dve.wait_ge(decayed_ready, (n + 1) // 2)
                    dve.tensor_tensor(t64, bank4(banks[7]), t32s(c, g), ALU.add).then_inc(t64_ready, 1)
                    dve.wait_ge(u_mm, 2 * n + 1)
                    if n:
                        dve.wait_ge(state_mm, (n + 1) // 2)
                        dve.wait_ge(o_ready, n)
                    dve.tensor_tensor(u64, bank4(banks[5]), u32s(c, g), ALU.add).then_inc(u_ready, 1)
                    if g + 1 < DKV:
                        convolve(q_step(g + 1, c))
                    dve.wait_ge(w_mm, 2 * n + 2)
                    join_rows(C["cross128"])
                    dve.wait_ge(u_mm, 2 * n + 2)
                    dve.wait_ge(u_ready, 2 * n + 1)
                    if n:
                        dve.wait_ge(gatedT_mm, n)
                    dve.tensor_tensor(u128, bank4(banks[5]), u64, ALU.add).then_inc(u_ready, 1)
                    if c == 1:
                        dve.wait_ge(ks_mm, g + 1)
                        dve.wait_ge(bv_ready, n + 1)
                        dve.wait_ge(ngb_ready, 1)
                        for r in range(DREP):
                            dve.scalar_tensor_tensor(rhs[:, r, :], banks[0][:, r * P:(r + 1) * P],
                                                     neg_gamma_beta[:, DREP * g + r:DREP * g + r + 1], rhs[:, r, :],
                                                     ALU.mult, ALU.add).then_inc(rhs_ready, 1)
                    dve.wait_ge(o_mm, n + 1)
                    if c == 1:
                        dve.wait_ge(qs_ready, DREP * (g + 1))
                        dve.tensor_tensor(o_gated, bank4(banks[6]), scaled, ALU.add).then_inc(o_ready, 1)
                    else:
                        dve.tensor_copy(flat(o_gated), banks[6]).then_inc(o_ready, 1)
                    dve.wait_ge(sum_q_ready, DREP * (n + 1))
                    if n:
                        dve.wait_ge(rms_step, 2 * n)
                    dve.tensor_scalar(rms_a, sum_q, L2_EPS, DK * LN_EPS, ALU.add, ALU.mult).then_inc(rms_step, 1)
                    dve.wait_ge(sum_o_ready, DREP * (n + 1))
                    dve.wait_ge(rms_step, 2 * n + 1)
                    if n:
                        dve.wait_ge(rms_ready, n)
                    dve.scalar_tensor_tensor(rms_b, sum_o, 1.0 / DK, rms_a, ALU.mult, ALU.add).then_inc(rms_step, 1)
                    dve.wait_ge(rms_ready, n + 1)
                    dve.wait_ge(silu_g_ready, n + 1)
                    for r in range(DREP):
                        dve.scalar_tensor_tensor(o_gated[:, r, :], o_gated[:, r, :], rms[:, r:r + 1], silu_g[:, r, :],
                                                 ALU.mult, ALU.mult).then_inc(gated_ready, 1)
                    dve.wait_ge(y_mm, n + 1)
                    dve.tensor_tensor(x[:, c, :], x[:, c, :], banks[0][:, 0:D], ALU.add).then_inc(x_added, 1)
        nc.sync.sem_clear(C["all_sems"])
        nc.all_engine_barrier()


def lut_layer(nc, C, ar, banks, x, x_out):
    ar.at = 0
    w = norm_buffers(ar)
    gate = [ar.take(SEQ) for _ in range(2)]
    hT = [ar.take(SEQ) for _ in range(2)]

    with ExitStack() as st:
        sem = lambda n: st.enter_context(nc.semaphore(n))
        stats, aggr, var_ready = sem("stats"), sem("aggr"), sem("var_ready")
        rstd_ready, xn_ready, xnT_psum, xnT_ready = sem("rstd_ready"), sem("xn_ready"), sem("xnT_psum"), sem("xnT_ready")
        up_mm, gate_ready, hT_ready, down_mm, x_done, stored = (
            sem("up_mm"), sem("gate_ready"), sem("hT_ready"), sem("down_mm"), sem("x_done"), sem("stored"))
        with nc.Block() as block:
            @block.sync
            def _(sp):
                sp.wait_ge(x_done, NT)
                sp.dma_start(x_out, x[:, :, :]).then_inc(stored, 16)
                sp.wait_ge(stored, 16)

            @block.gpsimd
            def _(pool):
                norm_rstd(pool, C, w, var_ready, rstd_ready)

            @block.tensor
            def _(pe):
                norm_transpose(pe, C, w, banks[0], xn_ready, xnT_psum)
                pe.wait_ge(xnT_ready, 1)

                def up(n):
                    rows = min(P, FI - n * P)
                    if n >= 2:
                        pe.wait_ge(hT_ready, n - 1)
                    for half in range(2):
                        for k in range(KD):
                            mm = pe.matmul(banks[2 + n % 2][0:rows, half * SEQ:(half + 1) * SEQ],
                                           C["ffn_gu"][:, k, half, n * P:n * P + rows], w["xnT"][:, k, :],
                                           start=(k == 0), stop=(k == KD - 1))
                    mm.then_inc(up_mm, 1)

                def down(n):
                    rows = min(P, FI - n * P)
                    pe.wait_ge(hT_ready, n + 1)
                    for t in range(NT):
                        mm = pe.matmul(banks[4 + t][:, 0:D], hT[n % 2][0:rows, t * P:(t + 1) * P],
                                       C["ffn_down"][0:rows, n, :], start=(n == 0), stop=(n == FTILES - 1))
                    mm.then_inc(down_mm, 1)

                up(0)
                for n in range(FTILES):
                    if n + 1 < FTILES:
                        up(n + 1)
                    down(n)

            @block.scalar
            def _(act):
                norm_copy(act, w, banks[0], xnT_psum, xnT_ready)
                for n in range(FTILES):
                    rows = min(P, FI - n * P)
                    act.wait_ge(up_mm, n + 1)
                    if n >= 2:
                        act.wait_ge(hT_ready, n - 1)
                    act.activation(gate[n % 2][0:rows], banks[2 + n % 2][0:rows, 0:SEQ], ACT.Silu).then_inc(gate_ready, 1)

            @block.vector
            def _(dve):
                norm_stats(dve, x, w, stats, aggr, var_ready)
                norm_apply(dve, x, w, rstd_ready, xn_ready)
                for n in range(FTILES):
                    rows = min(P, FI - n * P)
                    dve.wait_ge(gate_ready, n + 1)
                    if n >= 2:
                        dve.wait_ge(down_mm, n - 1)
                    dve.tensor_tensor(hT[n % 2][0:rows], gate[n % 2][0:rows], banks[2 + n % 2][0:rows, SEQ:2 * SEQ],
                                      ALU.mult).then_inc(hT_ready, 1)
                dve.wait_ge(down_mm, FTILES)
                for t in range(NT):
                    dve.tensor_tensor(x[:, t, :], x[:, t, :], banks[4 + t][:, 0:D], ALU.add).then_inc(x_done, 1)
        nc.sync.sem_clear(C["all_sems"])
        nc.all_engine_barrier()


def build(nc, io, out):
    n_seq = io["x"].shape[0]
    with ExitStack() as st:
        sb = lambda name, shape, dt=F32: st.enter_context(nc.sbuf_tensor(name, shape, dt))
        x = sb("x", [P, NT, D])
        C = {}
        loads = []

        def weight(name, shape, src):
            t = sb(name, [P] + shape)
            C[name] = t[(slice(None),) * (1 + len(shape))]
            loads.append((C[name], src))

        halves = lambda ap: ap.rearrange("(k p) n -> p k n", p=P)
        weight("ident", [P], io["ident"])
        weight("wqkv", [KD, NQKV], halves(io["wqkvT"]))
        weight("wo", [KD, D], halves(io["woT"]))
        weight("rope_cos", [NT, NROPE], io["rope_cos"].rearrange("(t p) n -> p t n", p=P))
        weight("rope_sin", [NT, NROPE], io["rope_sin"].rearrange("(t p) n -> p t n", p=P))
        weight("causal", [NSUB, SUB], io["causal"].rearrange("p (u k) -> p u k", k=SUB))
        weight("repeat_rows", [REP], io["repeat_rows"])
        weight("router", [KD, NE], halves(io["routerT"]))
        weight("earlier", [NE, NE], io["earlier"].rearrange("p (a b) -> p a b", b=NE))
        weight("gate_up", [KD, NE + 1, 2, INTER], io["gate_up"].rearrange("(k p) e h n -> p k e h n", p=P))
        weight("down", [NE + 1, D], io["down"].rearrange("e p n -> p e n"))
        weight("qkv_w", [KD, (DH + 2 * DKV) * DK], halves(io["qkv_wT"]))
        weight("conv_w", [DH + 2 * DKV, TAPS], io["conv_w"].rearrange("(c p) i -> p c i", p=P))
        weight("g_w", [KD, DH * DK], halves(io["g_wT"]))
        weight("bgk_w", [KD, 2 * DH], halves(io["bgk_wT"]))
        weight("o_w", [DH, D], io["o_wT"].rearrange("(h p) n -> p h n", p=P))
        weight("norm_w", [1], io["norm_w"].rearrange("(p a) -> p a", a=1))
        weight("lut", [LUT], io["lut"].rearrange("(a n) -> a n", a=1).broadcast_to([P, LUT]))
        weight("incl", [P], io["incl"])
        weight("later", [P], io["later"])
        weight("cross64", [P], io["cross64"])
        weight("cross128", [P], io["cross128"])
        weight("before", [P], io["before"])
        C["ffn_gu"] = sb("ffn_gu", [P, KD, 2, FI])[:, :, :, :]
        C["ffn_down"] = sb("ffn_down", [P, FTILES, D])[:, :, :]
        C["v32"] = sb("v32", [P, NT, NKV, 32])[:, :, :, :]
        C["bd"] = sb("bd", [P, HEAD_TILES * REP * GROUPS * SEQ])[:, :]
        C["tri_inv"] = sb("tri_inv", [P, SUB * SUB])[:, :]
        C["neg_half"] = sb("neg_half", [P, 8])[:, :]
        C["comb"] = sb("comb", [P, NT, NE + 1])[:, :, :]
        C["ones"] = sb("ones", [P, SUB])[:, :]
        size = WORK
        ar = Arena(sb("work", [P, size]), size)
        psum_scores = st.enter_context(nc.psum_tensor("psum_scores", [P, 3 * 512], F32))
        banks = [psum_scores[:, i * 512:(i + 1) * 512] for i in range(3)]
        banks += [st.enter_context(nc.psum_tensor(f"bank{i}", [P, 512], F32))[:, :] for i in range(3, 8)]
        C["psum_scores"] = psum_scores[:, :]
        chunks = []
        for half, name in enumerate(("gate_idxT", "up_idxT")):
            for k in range(KD):
                chunks.append((P, C["ffn_gu"][:, k, half, :], io[name][k * P:(k + 1) * P, :], FI))
        for i in range(FTILES):
            rows = min(P, FI - i * P)
            chunks.append((rows, C["ffn_down"][0:rows, i, :], io["down_idxT"][i * P:i * P + rows, :], D))
        C["ident_bf"] = sb("ident_bf", [P, P], BF16)[:, :]
        C["before_bf"] = sb("before_bf", [P, P], BF16)[:, :]
        scratch_dram = lambda name, shape: nc.dram_tensor(name, shape, F32, kind="Internal").ap()
        dram = {"bg": scratch_dram("scratch_bg", [2 * DH, SEQ]), "kk": scratch_dram("scratch_kk", [DKV, NSUB, SUB, SUB]),
                "t": scratch_dram("scratch_t", [DH * NSUB, SUB, SUB]), "u": scratch_dram("scratch_u", [DH * NSUB, SUB, SUB])}
        C["loads"], C["lut_chunks"] = loads, chunks
        scratch = {"idx": [ar.take(FI).bitcast(I32) for _ in range(2)], "term": [ar.take(FI) for _ in range(2)]}
        with ExitStack() as s2:
            first = s2.enter_context(nc.semaphore("first")).num
        C["all_sems"] = range(first, 256)
        load_weights(nc, None, sb, C, scratch)
        with nc.Fori(0, n_seq) as b:
            x_in = io["x"][bass.ds(b, 1)].rearrange("o (t p) n -> p (o t) n", p=P)
            x_out = out[bass.ds(b, 1)].rearrange("o (t p) n -> p (o t) n", p=P)
            attention_layer(nc, C, ar, banks, x, x_in)
            experts_layer(nc, C, ar, banks, x)
            delta_layer(nc, C, ar, banks, x, dram)
            lut_layer(nc, C, ar, banks, x, x_out)


def constants():
    i = np.arange(P)
    inv_freq = (1.0 / np.float32(10000.0) ** (np.arange(0, HD, 2, dtype=np.float32) / np.float32(HD))).astype(np.float32)
    freqs = np.outer(np.arange(SEQ, dtype=np.float32), inv_freq).astype(np.float32)
    cos, sin = np.cos(freqs), np.sin(freqs)
    cos = np.stack([cos, cos], -1).reshape(SEQ, HD)
    sin = np.stack([-sin, sin], -1).reshape(SEQ, HD)
    scale = np.concatenate([np.full(NH * HD, -(HD ** -0.5)), np.ones(NKV * HD)]).astype(np.float32)
    sub = i // SUB
    return {
        "ident": np.eye(P, dtype=np.float32),
        "rope_cos": np.tile(cos, (1, NH + NKV)).astype(np.float32) * scale,
        "rope_sin": np.tile(sin, (1, NH + NKV)).astype(np.float32) * scale,
        "causal": np.concatenate([np.zeros((P, P)), np.where(i[None, :] > i[:, None], BIG, 0.0)], 1).astype(np.float32),
        "repeat_rows": (i[:, None] % 32 // HD == np.arange(REP)[None, :]).astype(np.float32),
        "earlier": np.tile((np.arange(NE)[None, :] < np.arange(NE)[:, None]).reshape(1, -1), (P, 1)).astype(np.float32),
        "incl": (i[:, None] <= i[None, :]).astype(np.float32),
        "later": (i[:, None] > i[None, :]).astype(np.float32),
        "cross64": ((sub[:, None] // 2 == sub[None, :] // 2) & (sub[:, None] > sub[None, :])).astype(np.float32),
        "cross128": ((i[:, None] >= 64) & (i[None, :] < 64)).astype(np.float32),
        "before": np.where(i[:, None] > i[None, :], -BEFORE, 0.0).astype(np.float32),
    }


def host_layout(inp):
    a = {k: np.asarray(v) for k, v in inp.items()}
    T = lambda m: np.ascontiguousarray(m.T)
    gate = np.concatenate([a["L0_ffn_Wg"], a["L0_ffn_Wg_s"][None]], 0)
    up = np.concatenate([a["L0_ffn_Wu"], a["L0_ffn_Wu_s"][None]], 0)
    return {
        "x": a["L0_attn_x"],
        "wqkvT": T(np.concatenate([a["L0_attn_wq"], a["L0_attn_wk"], a["L0_attn_wv"]], 0)),
        "woT": T(a["L0_attn_wo"]),
        "routerT": T(a["L0_ffn_Wr"]),
        "gate_up": np.ascontiguousarray(np.stack([gate, up], 0).transpose(2, 1, 0, 3)),
        "down": np.concatenate([a["L0_ffn_Wd"], a["L0_ffn_Wd_s"][None]], 0),
        "qkv_wT": T(a["L1_attn_qkv_w"]),
        "conv_w": a["L1_attn_conv_w"],
        "g_wT": T(a["L1_attn_g_w"]),
        "bgk_wT": T(np.concatenate([a["L1_attn_b_w"], a["L1_attn_gk_w"]], 0)),
        "o_wT": T(a["L1_attn_o_w"]),
        "norm_w": a["L1_attn_out_norm_w"],
        "lut": a["L1_ffn_lut"],
        "gate_idxT": T(a["L1_ffn_gate_idx"]),
        "up_idxT": T(a["L1_ffn_up_idx"]),
        "down_idxT": T(a["L1_ffn_down_idx"]),
    }


def kernel(**inputs):
    import concourse.bacc as bacc
    from concourse.bass_utils import run_bass_kernel_spmd

    arrays = host_layout(inputs)
    arrays.update(constants())
    nc = bacc.Bacc("TRN2", target_bir_lowering=False, num_devices=1)
    io = {n: nc.dram_tensor(f"in_{n}", a.shape, mybir.dt.from_np(a.dtype), kind="ExternalInput").ap()
          for n, a in arrays.items()}
    out = nc.dram_tensor("out", arrays["x"].shape, F32, kind="ExternalOutput").ap()
    build(nc, io, out)
    result = run_bass_kernel_spmd(nc, [{f"in_{n}": a for n, a in arrays.items()}], core_ids=[0])
    return result.results[0]["out"]
```

```python
from contextlib import ExitStack

import numpy as np

import concourse.bass as bass
from concourse import mybir
from concourse.alu_op_type import AluOpType as ALU

F32 = mybir.dt.float32
BF16 = mybir.dt.bfloat16
I32 = mybir.dt.int32
ACT = mybir.ActivationFunctionType
AX = mybir.AxisListType

P = 128
D = 256
KD = D // P
SEQ = 256
NT = SEQ // P
LN_EPS = 1e-5

NH, NKV, HD = 32, 8, 8
NQKV = NH * HD + 2 * NKV * HD
NROPE = NH * HD + NKV * HD
REP = NH // NKV
GROUPS = 4
HEAD_TILES = NH * HD // P
BIG = 1e30

NE, INTER = 8, 128

DH, DKV, DK = 16, 4, 128
DREP = DH // DKV
SUB = 32
NSUB = SEQ // SUB
QB = P // SUB
TAPS = 4
L2_EPS = 1e-6

FI = 688
FTILES = (FI + P - 1) // P
LUT = 16

BEFORE = 30000.0
WORK = 14940


class Arena:

    def __init__(self, tensor, size):
        self.tensor, self.size, self.at = tensor, size, 0

    def take(self, *dims):
        n = 1
        for d in dims:
            n *= d
        assert self.at + n <= self.size, (self.at + n, self.size)
        flat = self.tensor[:, self.at:self.at + n]
        self.at += n
        names = "abcd"[:len(dims)]
        if len(dims) == 1:
            return flat
        return flat.rearrange(f"p ({' '.join(names)}) -> p {' '.join(names)}",
                              **{k: d for k, d in zip(names, dims)})


def spread(ap, axis, n):
    new = ap.unsqueeze(axis)
    shape = list(new.shape)
    shape[axis] = n
    return new.to_broadcast(shape)


def load_weights(nc, C, banks, scratch):
    with ExitStack() as st:
        sem = lambda n: st.enter_context(nc.semaphore(n))
        lut_loaded, loaded, zeroed, bd_zeroed = sem("lut_loaded"), sem("weights_loaded"), sem("zeroed"), sem("bd_zeroed")
        idx_loaded = [sem("indices_loaded_even"), sem("indices_loaded_odd")]
        term_ready, lut_sum, lut_mm, folded = sem("term_ready"), sem("lut_sum"), sem("lut_mm"), sem("norm_weight_folded")
        chunk_done = sem("chunk_done")
        first, loads, chunks = C["first_loads"], C["loads"], C["lut_chunks"]
        by_pe = [pe_adds for *_, pe_adds in chunks]
        pe_before = [sum(by_pe[:n]) for n in range(len(chunks) + 1)]
        terms = scratch["term"]
        with nc.Block() as block:
            @block.sync
            def _(sp):
                for dst, src in loads:
                    sp.dma_start(dst, src).then_inc(loaded, 16)
                sp.wait_ge(loaded, 16 * len(loads))

            @block.scalar
            def _(act):
                for dst, src in first:
                    act.dma_start(dst, src).then_inc(lut_loaded, 16)

                def load_indices(n):
                    rows, dst, src, width, _ = chunks[n]
                    if n >= 2:
                        act.wait_ge(term_ready, LUT * (n - 1))
                    act.dma_start(scratch["idx"][n % 2][0:rows, 0:width], src).then_inc(idx_loaded[n % 2], 16)

                load_indices(0)
                load_indices(1)
                for n, (rows, dst, src, width, _) in enumerate(chunks):
                    if n + 2 < len(chunks):
                        load_indices(n + 2)
                    if by_pe[n]:
                        half = width // 2
                        act.wait_ge(lut_mm, LUT * (pe_before[n] + 1))
                        for m in range(2):
                            act.activation(dst[:, m * half:(m + 1) * half], banks[2 * (pe_before[n] % 2) + m][0:rows, 0:half],
                                           ACT.Copy).then_inc(chunk_done, 1)

                act.wait_ge(loaded, 16 * len(loads))
                act.activation(C["o_w"], C["o_w"], ACT.Copy, scale=C["norm_w"]).then_inc(folded, 1)

            @block.tensor
            def _(pe):
                pe.wait_ge(lut_loaded, 16 * len(first))
                for n, (rows, dst, src, width, _) in enumerate(chunks):
                    if by_pe[n]:
                        half = width // 2
                        if pe_before[n] >= 2:
                            pe.wait_ge(chunk_done, 2 * (pe_before[n] - 1))
                        for v in range(LUT):
                            k = LUT * n + v
                            pe.wait_ge(term_ready, k + 1)
                            for m in range(2):
                                mm = pe.matmul(banks[2 * (pe_before[n] % 2) + m][0:rows, 0:half], C["ident"][0:rows, 0:rows],
                                               terms[k % len(terms)][0:rows, m * half:(m + 1) * half],
                                               start=(v == 0), stop=(v == LUT - 1))
                            mm.then_inc(lut_mm, 1)

            @block.gpsimd
            def _(pool):
                pool.memset(C["v32"], 0.0).then_inc(zeroed, 1)
                pool.wait_ge(zeroed, 1)
                pool.memset(C["v32"][:, :, :, HD:HD + 1], 1.0).then_inc(zeroed, 1)
                pool.memset(C["neg_half"], -0.5).then_inc(zeroed, 1)
                pool.memset(C["comb"], 1.0).then_inc(zeroed, 1)
                pool.memset(C["ones"], 1.0).then_inc(zeroed, 1)
                pool.memset(C["x_prev"], 0.0).then_inc(zeroed, 1)
                pool.memset(C["bd"], 0.0).then_inc(bd_zeroed, 1)

            @block.vector
            def _(dve):
                dve.wait_ge(lut_loaded, 16 * len(first))
                for n, (rows, dst, src, width, _) in enumerate(chunks):
                    idx = scratch["idx"][n % 2][0:rows, 0:width]
                    dve.wait_ge(idx_loaded[n % 2], 16 * (n // 2 + 1))
                    for v in range(LUT):
                        k = LUT * n + v
                        one = dst if v == 0 and not by_pe[n] else terms[k % len(terms)][0:rows, 0:width]
                        last = k - len(terms)
                        if last >= 0:
                            m, u = divmod(last, LUT)
                            if by_pe[m]:
                                dve.wait_ge(lut_mm, LUT * pe_before[m] + u + 1)
                            elif u:
                                dve.wait_ge(lut_sum, (LUT - 1) * (m - pe_before[m]) + u)
                        dve.tensor_scalar(one, idx, float(v), C["lut"][0:rows, v:v + 1],
                                          ALU.is_equal, ALU.mult).then_inc(term_ready, 1)
                        if v and not by_pe[n]:
                            dve.wait_ge(term_ready, k + 1)
                            if v > 1:
                                dve.wait_ge(lut_sum, (LUT - 1) * (n - pe_before[n]) + v - 1)
                            dve.tensor_tensor(dst, dst, one, ALU.add).then_inc(lut_sum, 1)
                dve.wait_ge(loaded, 16 * len(loads))
                dve.tensor_copy(C["before_bf"], C["before"])
                dve.tensor_copy(C["ident_bf"], C["ident"])
        nc.sync.sem_clear(C["all_sems"])
        nc.all_engine_barrier()


def norm_stats(dve, x, w, stats, aggr, var_ready):
    for t in range(NT):
        dve.bn_stats(w["bn6"][:, t, :], x[:, t, :]).then_inc(stats, 1)
    for t in range(NT):
        dve.wait_ge(stats, t + 1)
        dve.bn_aggr(w["mean_var"][:, t, :], w["bn6"][:, t, :]).then_inc(aggr, 1)
    dve.wait_ge(aggr, NT)
    dve.tensor_scalar(w["var_eps"], w["mean_var"][:, :, 1], LN_EPS, None, ALU.add).then_inc(var_ready, 1)


def norm_rstd(pool, C, w, var_ready, rstd_ready):
    pool.wait_ge(var_ready, 1)
    pool.tensor_tensor(w["rstd"], w["var_eps"], C["neg_half"][:, 0:NT], ALU.pow).then_inc(rstd_ready, 1)


def norm_apply(dve, x, w, rstd_ready, xn_ready):
    dve.wait_ge(rstd_ready, 1)
    for t in range(NT):
        dve.tensor_scalar(w["xn"][:, t, :], x[:, t, :], w["mean_var"][:, t, 0:1], w["rstd"][:, t:t + 1],
                          ALU.subtract, ALU.mult).then_inc(xn_ready, 1)


def norm_transpose(pe, C, w, bank, xn_ready, xnT_psum):
    for t in range(NT):
        pe.wait_ge(xn_ready, t + 1)
        for k in range(KD):
            mm = pe.transpose(bank[:, k * SEQ + t * P:k * SEQ + (t + 1) * P],
                              w["xn"][:, t, k * P:(k + 1) * P], C["ident"])
    mm.then_inc(xnT_psum, 1)


def norm_copy(act, w, bank, xnT_psum, xnT_ready):
    act.wait_ge(xnT_psum, 1)
    act.activation(w["xnT"].rearrange("p k n -> p (k n)"), bank[:], ACT.Copy).then_inc(xnT_ready, 1)


def norm_buffers(ar):
    return {"bn6": ar.take(NT, 6), "mean_var": ar.take(NT, 2), "var_eps": ar.take(NT), "rstd": ar.take(NT),
            "xn": ar.take(NT, D), "xnT": ar.take(KD, SEQ)}


def project_qkv(pe, C, xnT, banks, xnT_ready, qkv_mm):
    pe.wait_ge(xnT_ready, 1)
    for t in range(NT):
        for k in range(KD):
            mm = pe.matmul(banks[1 + t][:, 0:NQKV], xnT[:, k, t * P:(t + 1) * P], C["wqkv"][:, k, :],
                           start=(k == 0), stop=(k == KD - 1))
        mm.then_inc(qkv_mm, 1)


def first_projection(nc, C, ar, banks, x, x_in):
    ar.at = 0
    w = norm_buffers(ar)
    with ExitStack() as st:
        sem = lambda n: st.enter_context(nc.semaphore(n))
        x_loaded, stats, aggr, var_ready = sem("x_loaded"), sem("stats"), sem("aggr"), sem("var_ready")
        rstd_ready, xn_ready, xnT_psum, xnT_ready = sem("rstd_ready"), sem("xn_ready"), sem("xnT_psum"), sem("xnT_ready")
        qkv_mm = sem("qkv_mm")
        with nc.Block() as block:
            @block.sync
            def _(sp):
                sp.dma_start(x[:, :, :], x_in).then_inc(x_loaded, 16)

            @block.gpsimd
            def _(pool):
                norm_rstd(pool, C, w, var_ready, rstd_ready)

            @block.tensor
            def _(pe):
                norm_transpose(pe, C, w, banks[0], xn_ready, xnT_psum)
                project_qkv(pe, C, w["xnT"], banks, xnT_ready, qkv_mm)
                pe.wait_ge(qkv_mm, NT)

            @block.scalar
            def _(act):
                norm_copy(act, w, banks[0], xnT_psum, xnT_ready)

            @block.vector
            def _(dve):
                dve.wait_ge(x_loaded, 16)
                norm_stats(dve, x, w, stats, aggr, var_ready)
                norm_apply(dve, x, w, rstd_ready, xn_ready)
        nc.sync.sem_clear(C["all_sems"])
        nc.all_engine_barrier()


def attention_layer(nc, C, ar, banks, x):
    ar.at = 0
    qk = ar.take(NT, NROPE)
    swapped = ar.take(NT, NROPE)
    k_rep = ar.take(NT, HEAD_TILES, P)
    qT = ar.take(HEAD_TILES, SEQ)
    probs = [ar.take(GROUPS, 3 * P) for _ in range(2)]
    probsT = [ar.take(GROUPS, 3, P) for _ in range(2)]
    neg_max = [ar.take(2 * GROUPS) for _ in range(2)]
    outT = ar.take(SEQ)
    inv_sum = ar.take(NT, GROUPS)
    heads_out = ar.take(NT, D)
    headsT = ar.take(KD, SEQ)
    v32, keys, mask = C["v32"], C["bd"], C["causal"]
    units = HEAD_TILES * REP
    scores = C["psum_scores"]

    def keys_of(u):
        return keys[:, u * GROUPS * SEQ:(u + 1) * GROUPS * SEQ]

    with ExitStack() as st:
        sem = lambda n: st.enter_context(nc.semaphore(n))
        rope_cos, rope_sin, rope_done = sem("rope_cos"), sem("rope_sin"), sem("rope_done")
        v_ready, krep_ready, qT_psum, qT_ready = sem("v_ready"), sem("krep_ready"), sem("qT_psum"), sem("qT_ready")
        kT_psum, keys_dve, keys_act = sem("kT_psum"), sem("keys_dve"), sem("keys_act")
        scores_mm, masked, exp_done = sem("scores_mm"), sem("masked"), sem("exp_done")
        probsT_mm, probsT_dve, probsT_act = sem("probsT_mm"), sem("probsT_dve"), sem("probsT_act")
        pv_mm, outT_ready, out_mm, recip_done, out_done = sem("pv_mm"), sem("outT_ready"), sem("out_mm"), sem("recip_done"), sem("out_done")
        headsT_mm, headsT_ready, wo_mm, x_done = sem("headsT_mm"), sem("headsT_ready"), sem("wo_mm"), sem("x_done")
        with nc.Block() as block:
            @block.tensor
            def _(pe):
                for t in range(NT):
                    pe.wait_ge(rope_done, t + 1)
                    for i in range(HEAD_TILES):
                        mm = pe.transpose(banks[3][:, i * SEQ + t * P:i * SEQ + (t + 1) * P],
                                          qk[:, t, i * P:(i + 1) * P], C["ident"])
                mm.then_inc(qT_psum, 1)
                for t in range(NT):
                    pe.wait_ge(krep_ready, t + 1)
                    for i in range(HEAD_TILES):
                        mm = pe.transpose(banks[4 + i][:, t * P:(t + 1) * P], k_rep[:, t, i, :], C["ident"])
                mm.then_inc(kT_psum, 1)

                def score(u, rows):
                    i, r = divmod(u, REP)
                    if i == 0:
                        pe.wait_ge(keys_dve, GROUPS * (r + 1))
                    else:
                        pe.wait_ge(keys_act, GROUPS * (r + 1))
                    if u:
                        pe.wait_ge(masked, 2 * GROUPS * (u - 1) + GROUPS * (rows + 1))
                    half = GROUPS * P
                    for m in range(rows + 1):
                        mm = pe.matmul(scores[:, (rows + m) * half:(rows + m + 1) * half], qT[:, i, rows * P:(rows + 1) * P],
                                       keys_of(u)[:, m * half:(m + 1) * half], start=True, stop=True)
                    mm.then_inc(scores_mm, 1)

                def transpose_probs(u):
                    pe.wait_ge(exp_done, 2 * GROUPS * (u + 1))
                    if u == 0:
                        pe.wait_ge(keys_dve, GROUPS * REP)
                        pe.wait_ge(keys_act, GROUPS * REP)
                    else:
                        pe.wait_ge(probsT_dve, 2 * u)
                        pe.wait_ge(probsT_act, u)
                    for n in range(3 * GROUPS):
                        j, b = divmod(n, 3)
                        mm = pe.transpose(banks[3 + n // 4][:, n % 4 * P:(n % 4 + 1) * P],
                                          probs[u % 2][:, j, b * P:(b + 1) * P], C["ident"])
                        if n % 4 == 3:
                            mm.then_inc(probsT_mm, 1)

                def weigh_values(u):
                    i = u // REP
                    pe.wait_ge(probsT_dve, 2 * (u + 1))
                    pe.wait_ge(probsT_act, u + 1)
                    if u:
                        pe.wait_ge(outT_ready, u)
                    for j in range(GROUPS):
                        rows = slice(32 * j, 32 * j + 32)
                        pe.matmul(banks[6][rows, 0:SEQ], v32[:, 0, GROUPS * i + j, :],
                                  probsT[u % 2][:, j, 0:2, :].rearrange("p b n -> p (b n)"), start=True, stop=False,
                                  skip_group_check=True)
                        mm = pe.matmul(banks[6][rows, P:SEQ], v32[:, 1, GROUPS * i + j, :],
                                       probsT[u % 2][:, j, 2, :], start=False, stop=True, skip_group_check=True)
                    mm.then_inc(pv_mm, 1)

                def transpose_out(u):
                    pe.wait_ge(outT_ready, u + 1)
                    if u:
                        pe.wait_ge(out_done, u)
                    for t in range(NT):
                        mm = pe.transpose(banks[7][:, t * P:(t + 1) * P], outT[:, t * P:(t + 1) * P], C["ident"])
                    mm.then_inc(out_mm, 1)

                pe.wait_ge(qT_ready, 1)
                pe.wait_ge(v_ready, NT)
                score(0, 0)
                score(0, 1)
                for u in range(units + 3):
                    if u >= 3:
                        transpose_out(u - 3)
                    if 1 <= u <= units:
                        transpose_probs(u - 1)
                    if u + 1 < units:
                        score(u + 1, 0)
                    if 2 <= u < units + 2:
                        weigh_values(u - 2)
                    if u + 1 < units:
                        score(u + 1, 1)
                pe.wait_ge(out_done, units)
                for t in range(NT):
                    for k in range(KD):
                        mm = pe.transpose(banks[3][:, k * SEQ + t * P:k * SEQ + (t + 1) * P],
                                          heads_out[:, t, k * P:(k + 1) * P], C["ident"])
                mm.then_inc(headsT_mm, 1)
                pe.wait_ge(headsT_ready, 1)
                for t in range(NT):
                    for k in range(KD):
                        mm = pe.matmul(banks[4][:, t * D:(t + 1) * D], headsT[:, k, t * P:(t + 1) * P], C["wo"][:, k, :],
                                       start=(k == 0), stop=(k == KD - 1))
                mm.then_inc(wo_mm, 1)

            @block.scalar
            def _(act):
                act.wait_ge(qT_psum, 1)
                act.activation(qT.rearrange("p i n -> p (i n)"), banks[3][:], ACT.Copy).then_inc(qT_ready, 1)
                act.wait_ge(kT_psum, 1)
                for r in range(REP):
                    for j in range(GROUPS):
                        rows = slice(32 * j, 32 * j + 32)
                        act.activation(keys_of(REP + r)[rows].rearrange("p (u j k) -> p u j k", j=GROUPS, k=32)[:, :, j, :],
                                       banks[5][rows, 0:SEQ].rearrange("p (u k) -> p u k", k=32), ACT.Copy,
                                       scale=C["repeat_rows"][rows, r:r + 1]).then_inc(keys_act, 1)

                def exponentials(u, rows):
                    for j in range(GROUPS):
                        n = GROUPS * rows + j
                        cols = probs[u % 2][:, j, P:3 * P] if rows else probs[u % 2][:, j, 0:P]
                        act.wait_ge(masked, 2 * GROUPS * u + n + 1)
                        act.activation(cols, cols, ACT.Exp, bias=neg_max[u % 2][:, n:n + 1],
                                       scale=-1.0).then_inc(exp_done, 1)

                for u in range(units + 2):
                    if u < units:
                        exponentials(u, 0)
                    if 1 <= u <= units:
                        act.wait_ge(probsT_mm, 3 * u)
                        if u >= 3:
                            act.wait_ge(pv_mm, u - 2)
                        act.activation(probsT[(u - 1) % 2].rearrange("p j b n -> p (j b n)")[:, 8 * P:12 * P], banks[5][:],
                                       ACT.Copy).then_inc(probsT_act, 1)
                    if u < units:
                        exponentials(u, 1)
                    if u >= 2:
                        act.wait_ge(pv_mm, u - 1)
                        if u >= 3:
                            act.wait_ge(out_mm, u - 2)
                        act.activation(outT, banks[6][:, 0:SEQ], ACT.Copy).then_inc(outT_ready, 1)
                act.wait_ge(headsT_mm, 1)
                act.activation(headsT.rearrange("p k n -> p (k n)"), banks[3][:], ACT.Copy).then_inc(headsT_ready, 1)

            @block.vector
            def _(dve):
                for t in range(NT):
                    src = banks[1 + t]
                    heads = src[:, 0:NROPE].rearrange("p (h d) -> p h d", d=HD)
                    pairs = src[:, 0:NROPE].rearrange("p (h n c) -> p h n c", c=2, n=HD // 2)
                    sin = C["rope_sin"][:, t, :].rearrange("p (n c) -> p n c", c=2)
                    out = swapped[:, t, :].rearrange("p (h n c) -> p h n c", c=2, n=HD // 2)
                    dve.tensor_tensor(qk[:, t, :].rearrange("p (h d) -> p h d", d=HD), heads,
                                      spread(C["rope_cos"][:, t, :], 1, NH + NKV), ALU.mult).then_inc(rope_cos, 1)
                    for c in range(2):
                        dve.tensor_tensor(out[:, :, :, c], pairs[:, :, :, 1 - c], spread(sin[:, :, c], 1, NH + NKV),
                                          ALU.mult).then_inc(rope_sin, 1)
                    dve.tensor_copy(v32[:, t, :, 0:HD],
                                    src[:, NROPE:NQKV].rearrange("p (g d) -> p g d", d=HD)).then_inc(v_ready, 1)
                for t in range(NT):
                    dve.wait_ge(rope_sin, 2 * NT)
                    dve.tensor_tensor(qk[:, t, :], qk[:, t, :], swapped[:, t, :], ALU.add).then_inc(rope_done, 1)
                for t in range(NT):
                    dve.wait_ge(rope_done, NT)
                    for i in range(HEAD_TILES):
                        k4 = qk[:, t, NH * HD + i * 32:NH * HD + i * 32 + 32].rearrange("p (g d) -> p g d", d=HD)
                        last = dve.tensor_copy(k_rep[:, t, i, :].rearrange("p (g r d) -> p g r d", r=REP, d=HD),
                                               spread(k4, 2, REP))
                    last.then_inc(krep_ready, 1)
                dve.wait_ge(kT_psum, 1)
                for r in range(REP):
                    for j in range(GROUPS):
                        rows = slice(32 * j, 32 * j + 32)
                        dve.tensor_scalar(keys_of(r)[rows].rearrange("p (u j k) -> p u j k", j=GROUPS, k=32)[:, :, j, :],
                                          banks[4][rows, 0:SEQ].rearrange("p (u k) -> p u k", k=32),
                                          C["repeat_rows"][rows, r:r + 1], None, ALU.mult).then_inc(keys_dve, 1)

                def mask_max(u, rows):
                    dve.wait_ge(scores_mm, 2 * u + rows + 1)
                    if u >= 2:
                        dve.wait_ge(probsT_mm, 3 * (u - 1))
                    for j in range(GROUPS):
                        n = GROUPS * rows + j
                        if rows:
                            src, m, dst = scores[:, GROUPS * P:], mask[:, :, :], probs[u % 2][:, j, P:3 * P]
                        else:
                            src, m, dst = scores[:, 0:GROUPS * P], mask[:, 4:8, :], probs[u % 2][:, j, 0:P]
                        src = src.rearrange("p (u j k) -> p u j k", j=GROUPS, k=32)[:, :, j, :]
                        dve.tensor_tensor_reduce(dst.rearrange("p (u k) -> p u k", k=32), src, m, 1.0, 3.0e38, ALU.add, ALU.min,
                                                 neg_max[u % 2][:, n:n + 1]).then_inc(masked, 1)

                def copy_probs(u, m):
                    dve.wait_ge(probsT_mm, 3 * u + m + 1)
                    if u >= 2:
                        dve.wait_ge(pv_mm, u - 1)
                    dve.tensor_copy(probsT[u % 2].rearrange("p j b n -> p (j b n)")[:, m * 4 * P:(m + 1) * 4 * P],
                                    banks[3 + m][:]).then_inc(probsT_dve, 1)

                def normalise(u):
                    i, r = divmod(u, REP)
                    dve.wait_ge(out_mm, u + 1)
                    part = banks[7][:, 0:SEQ].rearrange("p (t j d) -> p t j d", t=NT, j=GROUPS)
                    dve.reciprocal(inv_sum, part[:, :, :, HD]).then_inc(recip_done, 1)
                    dve.wait_ge(recip_done, u + 1)
                    dst = heads_out.rearrange("p t (i j r d) -> p t i j r d", i=HEAD_TILES, j=GROUPS, r=REP)
                    dve.tensor_tensor(dst[:, :, i, :, r, :], part[:, :, :, 0:HD], spread(inv_sum, 3, HD),
                                      ALU.mult).then_inc(out_done, 1)

                for u in range(units + 3):
                    if u < units:
                        mask_max(u, 0)
                    if 1 <= u <= units:
                        copy_probs(u - 1, 0)
                    if u < units:
                        mask_max(u, 1)
                    if 1 <= u <= units:
                        copy_probs(u - 1, 1)
                    if u >= 3:
                        normalise(u - 3)
                dve.wait_ge(wo_mm, 1)
                dve.tensor_tensor(x[:, :, :], x[:, :, :], banks[4][:].rearrange("p (t n) -> p t n", t=NT),
                                  ALU.add).then_inc(x_done, 1)
        nc.sync.sem_clear(C["all_sems"])
        nc.all_engine_barrier()


def experts_layer(nc, C, ar, banks, x):
    ar.at = 0
    w = norm_buffers(ar)
    logits, shifted, weight = ar.take(NT, NE), ar.take(NT, NE), ar.take(NT, NE)
    above, level = ar.take(NT, NE, NE), ar.take(NT, NE, NE)
    rank, chosen = ar.take(NT, NE), ar.take(NT, NE)
    top, total, inv_total = ar.take(NT), ar.take(NT), ar.take(NT)
    gate = [ar.take(SEQ) for _ in range(2)]
    hT = [ar.take(SEQ) for _ in range(2)]
    comb = C["comb"]
    order = [NE] + list(range(NE))
    n_exp = len(order)

    with ExitStack() as st:
        sem = lambda n: st.enter_context(nc.semaphore(n))
        stats, aggr, var_ready = sem("stats"), sem("aggr"), sem("var_ready")
        rstd_ready, xn_ready, xnT_psum, xnT_ready = sem("rstd_ready"), sem("xn_ready"), sem("xnT_psum"), sem("xnT_ready")
        router_mm, route, exp_ready, comb_ready = sem("router_mm"), sem("route"), sem("exp_ready"), sem("comb_ready")
        up_mm, gate_ready, hT_ready, down_mm, x_added = sem("up_mm"), sem("gate_ready"), sem("hT_ready"), sem("down_mm"), sem("x_added")
        shift_ready = sem("shift_ready")
        with nc.Block() as block:
            @block.gpsimd
            def _(pool):
                norm_rstd(pool, C, w, var_ready, rstd_ready)

            @block.tensor
            def _(pe):
                norm_transpose(pe, C, w, banks[0], xn_ready, xnT_psum)
                pe.wait_ge(xnT_ready, 1)
                for t in range(NT):
                    for k in range(KD):
                        mm = pe.matmul(banks[1][:, t * NE:(t + 1) * NE], w["xnT"][:, k, t * P:(t + 1) * P],
                                       C["router"][:, k, :], start=(k == 0), stop=(k == KD - 1))
                mm.then_inc(router_mm, 1)

                def up(n):
                    e = order[n]
                    if n >= 2:
                        pe.wait_ge(hT_ready, n - 1)
                    for half in range(2):
                        for k in range(KD):
                            mm = pe.matmul(banks[2 + n % 2][:, half * SEQ:(half + 1) * SEQ],
                                           C["gate_up"][:, k, e, half, :], w["xnT"][:, k, :],
                                           start=(k == 0), stop=(k == KD - 1))
                    mm.then_inc(up_mm, 1)

                def down(n):
                    pe.wait_ge(hT_ready, n + 1)
                    if n >= 2:
                        pe.wait_ge(x_added, NT * (n - 1))
                    for t in range(NT):
                        mm = pe.matmul(banks[4 + n % 2][:, t * D:(t + 1) * D], hT[n % 2][:, t * P:(t + 1) * P],
                                       C["down"][:, order[n], :], start=True, stop=True)
                    mm.then_inc(down_mm, 1)

                up(0)
                for n in range(n_exp):
                    if n + 1 < n_exp:
                        up(n + 1)
                    down(n)

            @block.scalar
            def _(act):
                norm_copy(act, w, banks[0], xnT_psum, xnT_ready)
                act.wait_ge(shift_ready, 1)
                act.activation(weight, shifted, ACT.Exp).then_inc(exp_ready, 1)
                for n in range(n_exp):
                    act.wait_ge(up_mm, n + 1)
                    if n >= 2:
                        act.wait_ge(hT_ready, n - 1)
                    act.activation(gate[n % 2], banks[2 + n % 2][:, 0:SEQ], ACT.Silu).then_inc(gate_ready, 1)

            @block.vector
            def _(dve):
                norm_stats(dve, x, w, stats, aggr, var_ready)
                norm_apply(dve, x, w, rstd_ready, xn_ready)
                dve.wait_ge(router_mm, 1)
                steps = [0]

                def step(ins):
                    steps[0] += 1
                    ins.then_inc(route, 1)
                    dve.wait_ge(route, steps[0])

                step(dve.tensor_copy(logits, banks[1][:, 0:NT * NE].rearrange("p (t e) -> p t e", t=NT)))
                dve.tensor_reduce(top, logits, AX.X, ALU.max).then_inc(route, 1)
                steps[0] += 1
                dve.wait_ge(route, steps[0])
                dve.tensor_tensor(shifted, logits, spread(top, 2, NE), ALU.subtract).then_inc(shift_ready, 1)
                mine, others = spread(logits, 3, NE), spread(logits, 2, NE)
                step(dve.tensor_tensor(above, others, mine, ALU.is_gt))
                step(dve.tensor_tensor(level, others, mine, ALU.is_equal))
                step(dve.tensor_tensor(level, level, spread(C["earlier"], 1, NT), ALU.mult))
                step(dve.tensor_tensor(above, above, level, ALU.add))
                step(dve.tensor_reduce(rank, above, AX.X, ALU.add))
                step(dve.tensor_scalar(chosen, rank, 1.5, None, ALU.is_lt))
                dve.wait_ge(exp_ready, 1)
                step(dve.tensor_tensor(weight, weight, chosen, ALU.mult))
                step(dve.tensor_reduce(total, weight, AX.X, ALU.add))
                step(dve.reciprocal(inv_total, total))
                dve.tensor_tensor(comb[:, :, 0:NE], weight, spread(inv_total, 2, NE), ALU.mult).then_inc(comb_ready, 1)
                for n in range(n_exp + 1):
                    if n < n_exp:
                        dve.wait_ge(gate_ready, n + 1)
                        if n >= 2:
                            dve.wait_ge(down_mm, n - 1)
                        dve.tensor_tensor(hT[n % 2], gate[n % 2], banks[2 + n % 2][:, SEQ:2 * SEQ],
                                          ALU.mult).then_inc(hT_ready, 1)
                    if n:
                        e = order[n - 1]
                        dve.wait_ge(down_mm, n)
                        dve.wait_ge(comb_ready, 1)
                        for t in range(NT):
                            dve.wait_ge(x_added, NT * (n - 1))
                            dve.scalar_tensor_tensor(x[:, t, :], banks[4 + (n - 1) % 2][:, t * D:(t + 1) * D],
                                                     comb[:, t, e:e + 1], x[:, t, :], ALU.mult, ALU.add).then_inc(x_added, 1)
        nc.sync.sem_clear(C["all_sems"])
        nc.all_engine_barrier()


def delta_layer(nc, C, ar, banks, x, dram, x_prev, prev_out, next_in):
    ar.at = 0
    w = {"bn6": ar.take(NT, 6), "mean_var": ar.take(NT, 2), "var_eps": ar.take(NT), "rstd": ar.take(NT),
         "xnT": ar.take(KD, SEQ)}
    kT, kn0 = ar.take(DKV, SEQ), ar.take(DKV, P)
    v_tok, kk = ar.take(NT, DKV, P), ar.take(NT, DKV, P)
    conv = [ar.take(2, SEQ) for _ in range(2)]
    bg = ar.take(NT, 2 * DH)
    neg_beta, decay, neg_gamma_beta = ar.take(NT, DH), ar.take(2, DH), ar.take(DH)
    sum_k, k_eps, rnorm_k, junk = ar.take(NT, DKV), ar.take(NT, DKV), ar.take(NT, DKV), ar.take(P)
    sys_beta, sys_g, sys_c = ar.take(SUB), ar.take(SUB), ar.take(SUB)
    sum_q = [ar.take(DREP) for _ in range(2)]
    sum_o, rms_a, rms_b, rms = (ar.take(DREP) for _ in range(4))
    qT = [ar.take(DREP, SEQ) for _ in range(2)]
    k_raw, v_raw = qT
    prev = {"bn6": ar.take(NT, 6), "mean_var": ar.take(NT, 2), "var_eps": ar.take(NT), "rstd": ar.take(NT)}
    following = {"bn6": ar.take(NT, 6), "mean_var": ar.take(NT, 2), "var_eps": ar.take(NT), "rstd": ar.take(NT)}
    slot_at = ar.at
    slots = [ar.take(DREP, P) for _ in range(14)]
    g_incl, gamma, wt, bT, u64, rhs, delta, scaled, t32, state = slots[:10]
    probsT, u128 = slots[10:12], slots[12:14]
    t64, o_gated, o_gatedT = gamma, rhs, delta
    slot = lambda n, size: ar.tensor[:, slot_at + n * DREP * P:slot_at + n * DREP * P + size]
    rows_cols = lambda ap: ap.rearrange("p (i j) -> p i j", j=SUB)
    w["xn"] = slot(0, NT * D).rearrange("p (t n) -> p t n", t=NT)
    kn = [kn0, gamma]
    prev["xn"] = slot(11, NT * D).rearrange("p (t n) -> p t n", t=NT)
    prev["xnT"] = slot(9, KD * SEQ).rearrange("p (k n) -> p k n", k=KD)
    following["xnT"] = slot(12, KD * SEQ).rearrange("p (k n) -> p k n", k=KD)
    following["xn"] = slot(0, NT * D).rearrange("p (t n) -> p t n", t=NT)
    prev_gate = [v_raw[:, i, :] for i in range(2)]
    prev_hT = [v_raw[:, 2 + i, :] for i in range(2)]
    prev_step = {5 + 3 * n: n for n in range(FTILES)}
    bgT = slot(2, SEQ)
    sys_u, sys_d, sys_prod = rows_cols(slot(4, SUB * SUB)), rows_cols(slot(6, SUB * SUB)), slot(8, DREP * P)
    early = Arena(ar.tensor, ar.at)
    early.at = slot_at + 10 * DREP * P
    z, z_min, z_abs, e_abs, e_abs1 = (early.take(NT, 2 * DH) for _ in range(5))
    e_min, sig_den, log1 = early.take(NT, DH), early.take(NT, DH), early.take(NT, DH)
    bd = C["bd"].rearrange("p (u q j) -> p u q j", q=QB, j=SUB)
    flat = lambda ap: ap.rearrange("p a b -> p (a b)")
    per_head = lambda ap: spread(ap, 2, P)
    bank4 = lambda bank: bank.rearrange("p (r n) -> p r n", r=DREP)
    u32 = lambda c, h: C["bd"][:, (c * DH + h) * P:(c * DH + h + 1) * P]
    u32s = lambda c, g: bank4(C["bd"][:, (c * DH + DREP * g) * P:(c * DH + DREP * (g + 1)) * P])
    gate = lambda n: C["bd"][:, (NT * DH + DREP * n) * P:(NT * DH + DREP * (n + 1)) * P]
    units = [divmod(n, NT) for n in range(DKV * NT)]
    chunk = lambda c: slice(c * P, (c + 1) * P)

    tiles = [DH + n for n in range(2 * DKV)] + list(range(DH))
    step_tiles = [(tiles[2 * s], tiles[2 * s + 1]) for s in range(len(tiles) // 2)]
    q_step = lambda g, half: 4 + 2 * g + half

    def projected(s):
        if s < 2:
            return k_raw[:, 2 * s:2 * s + 2, :]
        if s < 4:
            return v_raw[:, 2 * s - 4:2 * s - 2, :]
        g, half = divmod(s - 4, 2)
        return qT[g % 2][:, 2 * half:2 * half + 2, :]

    gate_bank = [banks[0], banks[4]] + [banks[6 + n % 2] for n in range(2, len(units))]

    with ExitStack() as st:
        sem = lambda n: st.enter_context(nc.semaphore(n))
        stats, aggr, var_ready = sem("stats"), sem("aggr"), sem("var_ready")
        rstd_ready, xn_ready, xnT_psum, xnT_ready = sem("rstd_ready"), sem("xn_ready"), sem("xnT_psum"), sem("xnT_ready")
        proj_mm, conv_first, conv_step, silu_done = sem("proj_mm"), sem("conv_first"), sem("conv_step"), sem("silu_done")
        z_mm, gate_step, e_ready, log_ready, bg_ready = sem("z_mm"), sem("gate_step"), sem("e_ready"), sem("log_ready"), sem("bg_ready")
        c_mm, bgT_mm, decay_ready, bgT_ready, ngb_ready = sem("c_mm"), sem("bgT_mm"), sem("decay_ready"), sem("bgT_ready"), sem("ngb_ready")
        k_tok_mm, sum_k_ready, k_eps_ready, rnorm_ready = sem("k_tok_mm"), sem("sum_k_ready"), sem("k_eps_ready"), sem("rnorm_ready")
        kn_ready, kT_mm, kT_ready, kk_mm, kk_ready = sem("kn_ready"), sem("kT_mm"), sem("kT_ready"), sem("kk_mm"), sem("kk_ready")
        v_tok_mm, v_ready = sem("v_tok_mm"), sem("v_ready")
        kk_stored, bg_stored, sys_bg_loaded, sys_kk_loaded = sem("kk_stored"), sem("bg_stored"), sem("sys_bg_loaded"), sem("sys_kk_loaded")
        sys_step, sys_exp, inv_part = sem("sys_step"), sem("sys_exp"), [sem("inv_part_0"), sem("inv_part_1")]
        inv_steps = [2 * (SUB - 2), 2 * (SUB - 3)]
        next_loaded, next_stats, next_aggr, next_var_ready, next_rstd_ready = (
            sem("next_loaded"), sem("next_stats"), sem("next_aggr"), sem("next_var_ready"), sem("next_rstd_ready"))
        next_xn_ready, next_xnT_psum, next_xnT_ready, next_qkv_mm = (
            sem("next_xn_ready"), sem("next_xnT_psum"), sem("next_xnT_ready"), sem("next_qkv_mm"))
        u_stored, u_loaded = sem("u_stored"), [sem("u_loaded_0"), sem("u_loaded_1")]
        t32_mm, t32_ready, gate_mm, gate_zeroed = sem("t32_mm"), sem("t32_ready"), sem("gate_mm"), sem("gate_zeroed")
        g_ready, d_mm, gamma_ready, kq_mm, probs_ready, b_ready = (
            sem("g_ready"), sem("d_mm"), sem("gamma_ready"), sem("kq_mm"), sem("probs_ready"), sem("b_ready"))
        q_tok_mm, sum_q_ready, w_mm, w_ready = sem("q_tok_mm"), sem("sum_q_ready"), sem("w_mm"), sem("w_ready")
        t64_mm, t64_ready, u_mm, u_ready = sem("t64_mm"), sem("t64_ready"), sem("u_mm"), sem("u_ready")
        silu_g_ready, bv_ready, ks_mm, rhs_ready = sem("silu_g_ready"), sem("bv_ready"), sem("ks_mm"), sem("rhs_ready")
        delta_mm, delta_ready, decayed_ready, o_mm, qs_mm = sem("delta_mm"), sem("delta_ready"), sem("decayed_ready"), sem("o_mm"), sem("qs_mm")
        qs_ready, o_ready, sum_o_ready, rms_step, rms_ready = sem("qs_ready"), sem("o_ready"), sem("sum_o_ready"), sem("rms_step"), sem("rms_ready")
        gated_ready, gatedT_mm, gatedT_ready, y_mm, x_added = sem("gated_ready"), sem("gatedT_mm"), sem("gatedT_ready"), sem("y_mm"), sem("x_added")
        state_mm, state_ready = sem("state_mm"), sem("state_ready")
        prev_stats, prev_aggr, prev_var_ready, prev_rstd_ready = (
            sem("prev_stats"), sem("prev_aggr"), sem("prev_var_ready"), sem("prev_rstd_ready"))
        prev_xn_ready, prev_xnT_psum, prev_xnT_ready = sem("prev_xn_ready"), sem("prev_xnT_psum"), sem("prev_xnT_ready")
        prev_up_mm, prev_gate_ready, prev_hT_ready, prev_down_mm, prev_done, prev_stored = (
            sem("prev_up_mm"), sem("prev_gate_ready"), sem("prev_hT_ready"), sem("prev_down_mm"), sem("prev_done"), sem("prev_stored"))

        with nc.Block() as block:
            @block.sync
            def _(sp):
                sp.wait_ge(bgT_ready, 1)
                sp.dma_start(dram["bg"], bgT[0:2 * DH, :]).then_inc(bg_stored, 16)
                sp.wait_ge(bg_stored, 16)
                sp.dma_start(sys_beta, dram["bg"][0:DH].rearrange("h (b i) -> (h b) i", i=SUB)).then_inc(sys_bg_loaded, 16)
                sp.dma_start(sys_g, dram["bg"][DH:2 * DH].rearrange("h (b i) -> (h b) i", i=SUB)).then_inc(sys_bg_loaded, 16)
                for c in range(NT):
                    sp.wait_ge(kk_ready, c + 1)
                    for q in range(QB):
                        rows = slice(SUB * q, SUB * q + SUB)
                        sp.dma_start(dram["kk"].rearrange("g b i j -> b i g j")[c * QB + q],
                                     kk[rows, c, :, rows]).then_inc(kk_stored, 16)
                sp.wait_ge(kk_stored, 16 * NT * QB)
                sys_rows = sys_u.rearrange("p i j -> p (i j)")
                for g in range(DKV):
                    at = g * DREP * NSUB
                    sp.dma_start(sys_rows[at:at + DREP * NSUB],
                                 spread(dram["kk"][g].rearrange("b i j -> b (i j)"), 0, DREP)).then_inc(sys_kk_loaded, 16)
                for part in range(2):
                    sp.wait_ge(inv_part[part], inv_steps[part])
                sp.dma_start(dram["u"], sys_u).then_inc(u_stored, 16)
                sp.wait_ge(u_stored, 16)
                src = dram["u"].rearrange("(h c q) i j -> c q i h j", c=NT, q=QB)
                for c in range(NT):
                    for q in range(QB):
                        sp.dma_start(bd[SUB * q:SUB * q + SUB, c * DH:(c + 1) * DH, q, :], src[c, q]).then_inc(u_loaded[c], 16)
                sp.wait_ge(prev_done, NT)
                sp.dma_start(prev_out, x_prev[:, :, :]).then_inc(prev_stored, 16)
                sp.wait_ge(prev_stored, 16)
                sp.wait_ge(x_added, NT)
                sp.dma_start(x[:, :, :], next_in).then_inc(next_loaded, 16)

            @block.gpsimd
            def _(pool):
                norm_rstd(pool, C, w, var_ready, rstd_ready)
                norm_rstd(pool, C, prev, prev_var_ready, prev_rstd_ready)
                pool.wait_ge(sum_k_ready, NT * DKV)
                pool.tensor_scalar(flat(k_eps), flat(sum_k), L2_EPS, None, ALU.add).then_inc(k_eps_ready, 1)
                pool.wait_ge(k_eps_ready, 1)
                pool.tensor_tensor(flat(rnorm_k), flat(k_eps), C["neg_half"], ALU.pow).then_inc(rnorm_ready, 1)

                def masked_decays(f):
                    g, c = units[f]
                    pool.wait_ge(bg_ready, 1)
                    pool.wait_ge(xnT_psum, 1)
                    if f:
                        pool.wait_ge(d_mm, f)
                    pool.tensor_tensor(g_incl, spread(C["incl"], 1, DREP),
                                       per_head(bg[:, c, DH + DREP * g:DH + DREP * (g + 1)]), ALU.mult).then_inc(g_ready, 1)

                def decayed_kk(f):
                    g, c = units[f]
                    pool.wait_ge(gamma_ready, f + 1)
                    pool.wait_ge(kk_ready, NT)
                    if f:
                        pool.wait_ge(w_mm, 2 * f)
                    pool.tensor_tensor(bT, spread(kk[:, c, g, :], 1, DREP), gamma, ALU.mult).then_inc(b_ready, 1)

                masked_decays(0)
                decayed_kk(0)
                masked_decays(1)
                for part in range(2):
                    pool.wait_ge(inv_part[part], inv_steps[part])
                pool.wait_ge(u_stored, 16)
                for n, (g, c) in enumerate(units):
                    heads = slice(DREP * g, DREP * (g + 1))
                    if n:
                        pool.wait_ge(gatedT_mm, n)
                    pool.wait_ge(v_ready, NT)
                    pool.tensor_tensor(rhs, spread(v_tok[:, c, g, :], 1, DREP), per_head(bg[:, c, heads]),
                                       ALU.mult).then_inc(bv_ready, 1)
                    if n + 1 < len(units):
                        decayed_kk(n + 1)
                    if c == 0:
                        pool.wait_ge(decay_ready, 1)
                        pool.wait_ge(delta_ready, n + 1)
                        if n:
                            pool.wait_ge(o_ready, n)
                        pool.tensor_tensor(scaled, delta, per_head(decay[:, 1, heads]), ALU.mult).then_inc(decayed_ready, 1)
                    if n + 2 < len(units):
                        masked_decays(n + 2)
                    if n == len(units) - 1:
                        norm_rstd(pool, C, following, next_var_ready, next_rstd_ready)
                    pool.wait_ge(rms_step, 2 * (n + 1))
                    pool.tensor_tensor(rms, rms_b, C["neg_half"][:, 0:DREP], ALU.pow).then_inc(rms_ready, 1)
                    pool.wait_ge(gated_ready, DREP * (n + 1))
                    pool.memset(gate(n), 0.0).then_inc(gate_zeroed, 1)

            @block.tensor
            def _(pe):
                def project(s):
                    if s >= 2:
                        pe.wait_ge(conv_step, 6 * (s - 1))
                    for i, tile in enumerate(step_tiles[s]):
                        for k in range(KD):
                            mm = pe.matmul(banks[2 + s % 2][:, i * SEQ:(i + 1) * SEQ], C["qkv_w"][:, k, tile * P:(tile + 1) * P],
                                           w["xnT"][:, k, :], start=(k == 0), stop=(k == KD - 1))
                    mm.then_inc(proj_mm, 1)

                def decays(f):
                    pe.wait_ge(g_ready, f + 1)
                    if f:
                        pe.wait_ge(w_ready, 2 * DREP * f)
                    pe.matmul(banks[0], C["later"], flat(g_incl), start=True, stop=False)
                    pe.matmul(bank4(banks[0]), C["ident_bf"], spread(C["before_bf"], 1, DREP),
                              start=False, stop=True).then_inc(d_mm, 1)

                def scores(f):
                    g, c = units[f]
                    q = qT[g % 2]
                    pe.wait_ge(silu_done, 2 * (q_step(g, 1) + 1))
                    pe.wait_ge(kT_ready, NT)
                    if f:
                        pe.wait_ge(t32_ready, f + 1)
                    else:
                        pe.wait_ge(decay_ready, 1)
                    pe.matmul(bank4(banks[1]), kT[:, g, chunk(c)], q[:, :, chunk(c)], start=True, stop=True).then_inc(kq_mm, 1)
                    if f:
                        pe.wait_ge(u_ready, 2 * f)
                    else:
                        pe.wait_ge(kk_ready, NT)
                    for r in range(DREP):
                        mm = pe.transpose(banks[5][:, r * P:(r + 1) * P], q[:, r, chunk(c)], C["ident"])
                    mm.then_inc(q_tok_mm, 1)

                def transpose_u32(f):
                    g, c = units[f]
                    if f < NT:
                        pe.wait_ge(u_loaded[f], 16 * QB)
                    if f:
                        pe.wait_ge(t64_ready, f)
                    else:
                        pe.wait_ge(sum_q_ready, DREP)
                    for r in range(DREP):
                        mm = pe.transpose(banks[1 if f else 5][:, r * P:(r + 1) * P], u32(c, DREP * g + r), C["ident"])
                    mm.then_inc(t32_mm, 1)

                def joint(right):
                    for r in range(DREP):
                        mm = pe.matmul(banks[0][:, r * P:(r + 1) * P], bT[:, r, :], right(r), start=True, stop=True)
                    mm.then_inc(w_mm, 1)

                def join32(f):
                    g, c = units[f]
                    pe.wait_ge(b_ready, f + 1)
                    if f == 0:
                        pe.wait_ge(prev_done, NT)
                    pe.wait_ge(t32_ready, f + 1)
                    joint(lambda r: t32[:, r, :])

                def blocks64(f):
                    g, c = units[f]
                    pe.wait_ge(probs_ready, f + 1)
                    for r in range(DREP):
                        pe.wait_ge(w_ready, 2 * DREP * f + r + 1)
                        mm = pe.matmul(banks[1][:, r * P:(r + 1) * P], u32(c, DREP * g + r), wt[:, r, :], start=True, stop=True)
                    mm.then_inc(t64_mm, 1)
                    pe.wait_ge(sum_q_ready, DREP * (f + 1))
                    for r in range(DREP):
                        mm = pe.matmul(banks[5][:, r * P:(r + 1) * P], wt[:, r, :], u32(c, DREP * g + r), start=True, stop=True)
                    mm.then_inc(u_mm, 1)

                def join64(f):
                    pe.wait_ge(t64_ready, f + 1)
                    joint(lambda r: t64[:, r, :])

                def block128(f):
                    pe.wait_ge(u_ready, 2 * f + 1)
                    for r in range(DREP):
                        pe.wait_ge(w_ready, 2 * DREP * f + DREP + r + 1)
                        mm = pe.matmul(banks[5][:, r * P:(r + 1) * P], wt[:, r, :], u64[:, r, :], start=True, stop=True)
                    mm.then_inc(u_mm, 1)

                def open_gate(n):
                    g, c = units[n]
                    for k in range(KD):
                        mm = pe.matmul(gate_bank[n], w["xnT"][:, k, chunk(c)], C["g_w"][:, k, g * 512:(g + 1) * 512],
                                       start=(k == 0), stop=(k == KD - 1))
                    mm.then_inc(gate_mm, 1)

                norm_transpose(pe, C, w, banks[0], xn_ready, xnT_psum)
                pe.wait_ge(xnT_ready, 1)
                for t in range(NT):
                    for k in range(KD):
                        mm = pe.matmul(banks[1][:, t * 2 * DH:(t + 1) * 2 * DH], w["xnT"][:, k, chunk(t)],
                                       C["bgk_w"][:, k, :], start=(k == 0), stop=(k == KD - 1))
                mm.then_inc(z_mm, 1)
                norm_transpose(pe, C, prev, banks[6], prev_xn_ready, prev_xnT_psum)
                project(0)
                project(1)
                pe.wait_ge(bg_ready, 1)
                pe.matmul(banks[1][:, 64:64 + DH], C["incl"], bg[:, 1, DH:2 * DH], start=True, stop=True)
                pe.matmul(banks[1][:, 64 + DH:64 + 2 * DH], C["later"], bg[:, 0, DH:2 * DH],
                          start=True, stop=True).then_inc(c_mm, 1)
                for t in range(NT):
                    mm = pe.transpose(banks[7][0:2 * DH, chunk(t)], bg[:, t, :], C["ident"])
                mm.then_inc(bgT_mm, 1)
                open_gate(0)
                project(2)
                pe.wait_ge(silu_done, 4)
                pe.wait_ge(prev_xnT_ready, 1)
                for c in range(NT):
                    for g in range(DKV):
                        mm = pe.transpose(banks[5 + c][:, g * P:(g + 1) * P], k_raw[:, g, chunk(c)], C["ident"])
                    mm.then_inc(k_tok_mm, 1)
                open_gate(1)
                project(3)
                for c in range(NT):
                    pe.wait_ge(kn_ready, c + 1)
                    for g in range(DKV):
                        mm = pe.transpose(banks[5 + c][:, g * P:(g + 1) * P], kn[c][:, g, :], C["ident"])
                    mm.then_inc(kT_mm, 1)
                for c in range(NT):
                    pe.wait_ge(kT_ready, c + 1)
                    for g in range(DKV):
                        mm = pe.matmul(banks[5 + c][:, g * P:(g + 1) * P], kT[:, g, chunk(c)], kT[:, g, chunk(c)],
                                       start=True, stop=True)
                    mm.then_inc(kk_mm, 1)
                project(4)
                project(5)
                pe.wait_ge(silu_g_ready, 2)
                decays(0)
                pe.wait_ge(silu_done, 8)
                pe.wait_ge(bgT_ready, 1)
                for c in range(NT):
                    for g in range(DKV):
                        mm = pe.transpose(banks[4 if c == 0 else 7][:, g * P:(g + 1) * P], v_raw[:, g, chunk(c)], C["ident"])
                    mm.then_inc(v_tok_mm, 1)
                project(6)
                scores(0)
                project(7)

                def prev_up(n):
                    rows = min(P, FI - n * P)
                    if n >= 2:
                        pe.wait_ge(prev_hT_ready, n - 1)
                    for half in range(2):
                        for k in range(KD):
                            mm = pe.matmul(banks[6 + n % 2][0:rows, half * SEQ:(half + 1) * SEQ],
                                           C["ffn_gu"][:, k, half, n * P:n * P + rows], prev["xnT"][:, k, :],
                                           start=(k == 0), stop=(k == KD - 1))
                    mm.then_inc(prev_up_mm, 1)

                def prev_down(n):
                    rows = min(P, FI - n * P)
                    pe.wait_ge(prev_hT_ready, n + 1)
                    for t in range(NT):
                        mm = pe.matmul(banks[4 * t][:, 0:D], prev_hT[n % 2][0:rows, chunk(t)],
                                       C["ffn_down"][0:rows, n, :], start=(n == 0), stop=(n == FTILES - 1))
                    mm.then_inc(prev_down_mm, 1)

                pe.wait_ge(v_ready, NT)
                pe.wait_ge(kk_ready, NT)
                pe.wait_ge(gamma_ready, 1)
                prev_up(0)
                for n in range(FTILES):
                    if n + 1 < FTILES:
                        prev_up(n + 1)
                    prev_down(n)
                for n in range(2, len(units)):
                    pe.wait_ge(silu_g_ready, n - 1)
                    open_gate(n)
                transpose_u32(0)
                join32(0)
                blocks64(0)
                join64(0)
                block128(0)
                decays(1)
                transpose_u32(1)

                for n, (g, c) in enumerate(units):
                    q = qT[g % 2]
                    f = n + 1
                    if n:
                        pe.wait_ge(gatedT_ready, n)
                    else:
                        pe.wait_ge(silu_g_ready, len(units))
                    if c == 1:
                        pe.wait_ge(state_ready, g + 1)
                        pe.matmul(banks[6], kT[:, g, chunk(c)], flat(state), start=True, stop=True).then_inc(ks_mm, 1)
                    if f < len(units):
                        scores(f)
                    if c == 1:
                        pe.wait_ge(rhs_ready, DREP * (g + 1))
                    pe.wait_ge(u_ready, 2 * n + 2)
                    pe.wait_ge(bv_ready, n + 1)
                    for r in range(DREP):
                        mm = pe.matmul(banks[6][:, r * P:(r + 1) * P], u128[n % 2][:, r, :], rhs[:, r, :], start=True, stop=True)
                    mm.then_inc(delta_mm, 1)
                    if f < len(units):
                        join32(f)
                    if c == 1:
                        pe.wait_ge(x_added, n)
                        for r in range(DREP):
                            mm = pe.matmul(banks[4][:, r * P:(r + 1) * P], q[:, r, chunk(c)], state[:, r, :], start=True, stop=True)
                        mm.then_inc(qs_mm, 1)
                    pe.wait_ge(delta_ready, n + 1)
                    if n:
                        pe.wait_ge(o_ready, n)
                    for r in range(DREP):
                        mm = pe.matmul(banks[7][:, r * P:(r + 1) * P], probsT[n % 2][:, r, :], delta[:, r, :], start=True, stop=True)
                    mm.then_inc(o_mm, 1)
                    if f < len(units):
                        blocks64(f)
                    else:
                        norm_transpose(pe, C, following, banks[0], next_xn_ready, next_xnT_psum)
                        project_qkv(pe, C, following["xnT"], banks, next_xnT_ready, next_qkv_mm)
                    if c == 0:
                        pe.wait_ge(decayed_ready, g + 1)
                        if n:
                            pe.wait_ge(x_added, n)
                        pe.matmul(banks[4], kn0[:, g, :], flat(scaled), start=True, stop=True).then_inc(state_mm, 1)
                    if f < len(units):
                        join64(f)
                    if n + 8 < len(step_tiles):
                        project(n + 8)
                    if f < len(units):
                        block128(f)
                    for r in range(DREP):
                        pe.wait_ge(gated_ready, DREP * n + r + 1)
                        mm = pe.transpose(banks[6][:, r * P:(r + 1) * P], o_gated[:, r, :], C["ident"])
                    mm.then_inc(gatedT_mm, 1)
                    if f + 1 < len(units):
                        decays(f + 1)
                        transpose_u32(f + 1)
                    pe.wait_ge(gatedT_ready, n + 1)
                    if c == 1:
                        pe.wait_ge(qs_ready, DREP * (g + 1))
                    else:
                        pe.wait_ge(state_ready, g + 1)
                    for r in range(DREP):
                        mm = pe.matmul(banks[4][:, 0:D], o_gatedT[:, r, :], C["o_w"][:, DREP * g + r, :],
                                       start=(r == 0), stop=(r == DREP - 1))
                    mm.then_inc(y_mm, 1)

            @block.scalar
            def _(act):
                def conv_start(s):
                    act.wait_ge(proj_mm, s + 1)
                    if s >= 2:
                        act.wait_ge(silu_done, 2 * (s - 1))
                    for i, tile in enumerate(step_tiles[s]):
                        act.activation(conv[s % 2][:, i, :], banks[2 + s % 2][:, i * SEQ:(i + 1) * SEQ], ACT.Copy,
                                       scale=C["conv_w"][:, tile, TAPS - 1:TAPS]).then_inc(conv_first, 1)

                def conv_silu(s):
                    act.wait_ge(conv_step, 6 * (s + 1))
                    if s >= 8:
                        act.wait_ge(qs_mm, (s - 4) // 2 - 1)
                    elif s >= 6:
                        act.wait_ge(v_tok_mm, NT)
                        act.wait_ge(prev_down_mm, FTILES)
                    elif s >= 4:
                        act.wait_ge(k_tok_mm, NT)
                    for i in range(2):
                        act.activation(projected(s)[:, i, :], conv[s % 2][:, i, :], ACT.Silu).then_inc(silu_done, 1)

                def decay_exp(f):
                    act.wait_ge(d_mm, f + 1)
                    if f:
                        act.wait_ge(w_mm, 2 * f)
                    else:
                        act.wait_ge(kT_mm, NT)
                    act.activation(flat(gamma), banks[0], ACT.Exp).then_inc(gamma_ready, 1)

                def q_squares(f):
                    act.wait_ge(q_tok_mm, f + 1)
                    if f >= 2:
                        act.wait_ge(rms_step, 2 * (f - 1))
                    for r in range(DREP):
                        if f or r:
                            act.wait_ge(sum_q_ready, DREP * f + r)
                        if f >= 2:
                            act.wait_ge(sum_o_ready, DREP * (f - 1))
                        act.activation(junk, banks[5][:, r * P:(r + 1) * P], ACT.Square,
                                       accum_out=sum_q[f % 2][:, r:r + 1]).then_inc(sum_q_ready, 1)

                def open_gate(n):
                    act.wait_ge(gate_mm, n + 1)
                    act.activation(gate(n), gate_bank[n], ACT.Silu).then_inc(silu_g_ready, 1)

                norm_copy(act, w, banks[0], xnT_psum, xnT_ready)
                norm_copy(act, prev, banks[6], prev_xnT_psum, prev_xnT_ready)
                act.wait_ge(gate_step, 3)
                act.activation(e_abs, z_abs, ACT.Exp).then_inc(e_ready, 1)
                act.activation(e_min, z_min[:, :, 0:DH], ACT.Exp).then_inc(e_ready, 1)
                act.wait_ge(gate_step, 4)
                act.activation(log1, e_abs1[:, :, DH:2 * DH], ACT.Ln).then_inc(log_ready, 1)
                conv_start(0)
                conv_start(1)
                conv_silu(0)
                conv_silu(1)
                conv_start(2)
                for c in range(NT):
                    act.wait_ge(k_tok_mm, c + 1)
                    for g in range(DKV):
                        if c or g:
                            act.wait_ge(sum_k_ready, DKV * c + g)
                        act.activation(junk, banks[5 + c][:, g * P:(g + 1) * P], ACT.Square,
                                       accum_out=sum_k[:, c, g:g + 1]).then_inc(sum_k_ready, 1)
                open_gate(0)
                open_gate(1)
                conv_start(3)
                for c in range(NT):
                    act.wait_ge(kT_mm, c + 1)
                    act.activation(kT[:, :, chunk(c)], bank4(banks[5 + c]), ACT.Copy).then_inc(kT_ready, 1)
                conv_silu(2)
                conv_silu(3)
                conv_start(4)
                conv_start(5)
                act.wait_ge(c_mm, 1)
                act.activation(flat(decay), banks[1][:, 64:64 + 2 * DH], ACT.Exp).then_inc(decay_ready, 1)
                act.wait_ge(sys_step, 3)
                act.activation(sys_d, sys_d, ACT.Exp).then_inc(sys_exp, 1)
                decay_exp(0)
                for c in range(NT):
                    act.wait_ge(v_tok_mm, c + 1)
                    act.activation(flat(v_tok[:, c, :, :]), banks[4 if c == 0 else 7], ACT.Copy).then_inc(v_ready, 1)
                conv_silu(4)
                conv_silu(5)
                conv_start(6)
                conv_start(7)
                q_squares(0)
                for n in range(FTILES):
                    rows = min(P, FI - n * P)
                    act.wait_ge(prev_up_mm, n + 1)
                    if n >= 2:
                        act.wait_ge(prev_hT_ready, n - 1)
                    act.activation(prev_gate[n % 2][0:rows], banks[6 + n % 2][0:rows, 0:SEQ], ACT.Silu).then_inc(prev_gate_ready, 1)
                for n in range(2, len(units)):
                    open_gate(n)

                def copy_t32(f):
                    act.wait_ge(t32_mm, f + 1)
                    if f:
                        act.wait_ge(t64_ready, f)
                    act.activation(flat(t32), banks[1 if f else 5], ACT.Copy).then_inc(t32_ready, 1)

                copy_t32(0)
                for n, (g, c) in enumerate(units):
                    f = n + 1
                    if f < len(units):
                        decay_exp(f)
                    if n == 0:
                        copy_t32(1)
                    act.wait_ge(delta_mm, n + 1)
                    act.activation(flat(delta), banks[6], ACT.Copy).then_inc(delta_ready, 1)
                    if f < len(units):
                        q_squares(f)
                    if c == 1:
                        act.wait_ge(qs_mm, g + 1)
                        for r in range(DREP):
                            act.activation(scaled[:, r, :], banks[4][:, r * P:(r + 1) * P], ACT.Copy,
                                           scale=decay[:, 0, DREP * g + r:DREP * g + r + 1]).then_inc(qs_ready, 1)
                    if f == len(units):
                        norm_copy(act, following, banks[0], next_xnT_psum, next_xnT_ready)
                    act.wait_ge(o_ready, n + 1)
                    for r in range(DREP):
                        act.wait_ge(sum_q_ready, DREP * min(f + 1, len(units)))
                        if n or r:
                            act.wait_ge(sum_o_ready, DREP * n + r)
                        if n and r == 0:
                            act.wait_ge(rms_step, 2 * n)
                        act.activation(junk, o_gated[:, r, :], ACT.Square, accum_out=sum_o[:, r:r + 1]).then_inc(sum_o_ready, 1)
                    if c == 0:
                        act.wait_ge(state_mm, g + 1)
                        act.activation(flat(state), banks[4], ACT.Copy).then_inc(state_ready, 1)
                    if c == 0 and g + 1 < DKV:
                        conv_silu(q_step(g + 1, 0))
                        conv_silu(q_step(g + 1, 1))
                    if n + 8 < len(step_tiles):
                        conv_start(n + 8)
                    act.wait_ge(gatedT_mm, n + 1)
                    if c == 0:
                        act.wait_ge(decayed_ready, g + 1)
                    act.activation(flat(o_gatedT), banks[6], ACT.Copy).then_inc(gatedT_ready, 1)
                    if f + 1 < len(units):
                        copy_t32(f + 1)

            @block.vector
            def _(dve):
                def convolve_tap(s, tap):
                    back = TAPS - 1 - tap
                    for i, tile in enumerate(step_tiles[s]):
                        if tap:
                            dve.wait_ge(conv_step, 6 * s + 2 * (tap - 1) + i + 1)
                        y = conv[s % 2][:, i, back:SEQ]
                        dve.scalar_tensor_tensor(y, banks[2 + s % 2][:, i * SEQ:(i + 1) * SEQ - back],
                                                 C["conv_w"][:, tile, tap:tap + 1], y, ALU.mult, ALU.add).then_inc(conv_step, 1)

                def convolve(s):
                    dve.wait_ge(conv_first, 2 * (s + 1))
                    for tap in range(TAPS - 1):
                        convolve_tap(s, tap)

                def prev_product(n):
                    rows = min(P, FI - n * P)
                    dve.wait_ge(prev_gate_ready, n + 1)
                    if n >= 2:
                        dve.wait_ge(prev_down_mm, n - 1)
                    dve.tensor_tensor(prev_hT[n % 2][0:rows], prev_gate[n % 2][0:rows], banks[6 + n % 2][0:rows, SEQ:2 * SEQ],
                                      ALU.mult).then_inc(prev_hT_ready, 1)

                def decayed_scores(f):
                    dve.wait_ge(kq_mm, f + 1)
                    dve.wait_ge(gamma_ready, f + 1)
                    if f >= 2:
                        dve.wait_ge(o_mm, f - 1)
                    dve.tensor_tensor(probsT[f % 2], bank4(banks[1]), gamma, ALU.mult).then_inc(probs_ready, 1)

                def join_rows(f, mask):
                    g, c = units[f]
                    for r in range(DREP):
                        dve.scalar_tensor_tensor(wt[:, r, :], banks[0][:, r * P:(r + 1) * P],
                                                 neg_beta[:, c, DREP * g + r:DREP * g + r + 1], mask,
                                                 ALU.mult, ALU.mult).then_inc(w_ready, 1)

                def rows32(f):
                    dve.wait_ge(w_mm, 2 * f + 1)
                    if f:
                        dve.wait_ge(u_mm, 2 * f)
                    join_rows(f, C["cross64"])

                def blocks64(f):
                    g, c = units[f]
                    dve.wait_ge(t64_mm, f + 1)
                    dve.tensor_tensor(t64, bank4(banks[1]), t32, ALU.add).then_inc(t64_ready, 1)
                    dve.wait_ge(u_mm, 2 * f + 1)
                    if f:
                        dve.wait_ge(u_ready, 2 * f)
                    dve.tensor_tensor(u64, bank4(banks[5]), u32s(c, g), ALU.add).then_inc(u_ready, 1)

                def rows64(f):
                    dve.wait_ge(w_mm, 2 * f + 2)
                    join_rows(f, C["cross128"])

                def block128(f):
                    dve.wait_ge(u_mm, 2 * f + 2)
                    dve.wait_ge(u_ready, 2 * f + 1)
                    if f >= 2:
                        dve.wait_ge(delta_mm, f - 1)
                    dve.tensor_tensor(u128[f % 2], bank4(banks[5]), u64, ALU.add).then_inc(u_ready, 1)

                def add_output(n):
                    c = units[n][1]
                    dve.wait_ge(y_mm, n + 1)
                    if n < NT:
                        dve.wait_ge(prev_stored, 16)
                    dve.tensor_tensor(x_prev[:, c, :], (x if n < NT else x_prev)[:, c, :], banks[4][:, 0:D],
                                      ALU.add).then_inc(x_added, 1)

                norm_stats(dve, x, w, stats, aggr, var_ready)
                norm_stats(dve, x_prev, prev, prev_stats, prev_aggr, prev_var_ready)
                norm_apply(dve, x, w, rstd_ready, xn_ready)
                norm_apply(dve, x_prev, prev, prev_rstd_ready, prev_xn_ready)
                dve.wait_ge(z_mm, 1)
                dve.tensor_copy(flat(z), banks[1][:, 0:NT * 2 * DH]).then_inc(gate_step, 1)
                dve.wait_ge(gate_step, 1)
                dve.tensor_scalar(z_min, z, 0.0, None, ALU.min).then_inc(gate_step, 1)
                dve.scalar_tensor_tensor(flat(z_abs), flat(z), -1.0, flat(z), ALU.mult, ALU.min).then_inc(gate_step, 1)
                dve.wait_ge(e_ready, 2)
                dve.tensor_scalar(e_abs1, e_abs, 1.0, None, ALU.add).then_inc(gate_step, 1)
                dve.wait_ge(gate_step, 4)
                dve.reciprocal(sig_den, e_abs1[:, :, 0:DH]).then_inc(gate_step, 1)
                dve.wait_ge(log_ready, 1)
                dve.tensor_tensor(log1, z_min[:, :, DH:2 * DH], log1, ALU.subtract).then_inc(gate_step, 1)
                dve.wait_ge(gate_step, 6)
                dve.tensor_tensor(bg[:, :, 0:DH], e_min, sig_den, ALU.mult).then_inc(gate_step, 1)
                dve.wait_ge(gate_step, 7)
                dve.tensor_scalar(neg_beta, bg[:, :, 0:DH], -1.0, None, ALU.mult).then_inc(gate_step, 1)
                dve.wait_ge(gate_step, 8)
                dve.tensor_scalar(bg[:, :, DH:2 * DH], log1, 1.0 / 16.0, None, ALU.mult).then_inc(bg_ready, 1)
                convolve(0)
                convolve(1)
                dve.wait_ge(bgT_mm, 1)
                dve.tensor_copy(bgT[0:2 * DH, :], banks[7][0:2 * DH, 0:SEQ]).then_inc(bgT_ready, 1)
                convolve(2)
                dve.wait_ge(rnorm_ready, 1)
                for c in range(NT):
                    dve.tensor_tensor(kn[c], bank4(banks[5 + c]), per_head(rnorm_k[:, c, :]), ALU.mult).then_inc(kn_ready, 1)
                convolve(3)
                for c in range(NT):
                    dve.wait_ge(kk_mm, c + 1)
                    dve.tensor_tensor(kk[:, c, :, :], bank4(banks[5 + c]), spread(C["incl"], 1, DKV),
                                      ALU.mult).then_inc(kk_ready, 1)
                dve.wait_ge(sys_bg_loaded, 32)
                dve.tensor_tensor_scan(sys_c, C["ones"], sys_g, 0.0, ALU.mult, ALU.add).then_inc(sys_step, 1)
                dve.wait_ge(sys_step, 1)
                dve.tensor_tensor(sys_d, spread(sys_c, 1, SUB), spread(sys_c, 2, SUB), ALU.subtract).then_inc(sys_step, 1)
                dve.wait_ge(sys_step, 2)
                dve.tensor_scalar(sys_d, sys_d, 0.0, None, ALU.min).then_inc(sys_step, 1)
                convolve(4)
                dve.wait_ge(sys_exp, 1)
                dve.scalar_tensor_tensor(sys_d, sys_d, -1.0, spread(sys_beta, 1, SUB), ALU.mult, ALU.mult).then_inc(sys_step, 1)
                convolve(5)
                dve.wait_ge(sys_kk_loaded, 16 * DKV)
                dve.wait_ge(sys_step, 4)
                dve.tensor_tensor(sys_u, sys_u, sys_d, ALU.mult).then_inc(sys_step, 1)
                dve.wait_ge(sys_step, 5)
                dve.memset(sys_u.rearrange("p i j -> p (i j)")[:, 0:SUB * SUB:SUB + 1], 1.0).then_inc(sys_step, 1)
                dve.wait_ge(sys_step, 6)
                steps = [0, 0]

                def inverse_op(part, out, a, b, op):
                    dve.tensor_tensor(out, a, b, op).then_inc(inv_part[part], 1)
                    steps[part] += 1

                for j in range(1, SUB - 1):
                    mid = j + 1 + (SUB - j) // 2
                    if j > 1:
                        dve.wait_ge(inv_part[0], steps[0])
                    parts = [(0, j + 1, mid)] + ([(1, mid, SUB)] if mid < SUB else [])
                    prods = [sys_prod[:, 256 * part:256 * part + j * (end - at)].rearrange("p (c i) -> p c i", i=end - at)
                             for part, at, end in parts]
                    for part, at, end in parts:
                        if part and j > 1:
                            dve.wait_ge(inv_part[1], steps[1])
                        inverse_op(part, prods[part], spread(sys_u[:, j, at:end], 1, j), spread(sys_u[:, 0:j, j], 2, end - at), ALU.mult)
                    if j in prev_step:
                        prev_product(prev_step[j])
                    for part, at, end in parts:
                        dve.wait_ge(inv_part[part], steps[part])
                        inverse_op(part, sys_u[:, 0:j, at:end], sys_u[:, 0:j, at:end], prods[part], ALU.add)
                assert steps == inv_steps
                dve.wait_ge(decay_ready, 1)
                dve.tensor_tensor(neg_gamma_beta, neg_beta[:, 1, :], decay[:, 0, :], ALU.mult).then_inc(ngb_ready, 1)
                convolve(q_step(1, 0))
                convolve(q_step(1, 1))
                dve.wait_ge(prev_down_mm, FTILES)
                for t in range(NT):
                    dve.tensor_tensor(x_prev[:, t, :], x_prev[:, t, :], banks[4 * t][:, 0:D], ALU.add).then_inc(prev_done, 1)
                decayed_scores(0)
                rows32(0)
                blocks64(0)
                rows64(0)
                block128(0)

                for n, (g, c) in enumerate(units):
                    f = n + 1
                    if c == 1:
                        dve.wait_ge(ks_mm, g + 1)
                        dve.wait_ge(bv_ready, n + 1)
                        dve.wait_ge(ngb_ready, 1)
                        for r in range(DREP):
                            dve.scalar_tensor_tensor(rhs[:, r, :], banks[6][:, r * P:(r + 1) * P],
                                                     neg_gamma_beta[:, DREP * g + r:DREP * g + r + 1], rhs[:, r, :],
                                                     ALU.mult, ALU.add).then_inc(rhs_ready, 1)
                    if f < len(units):
                        decayed_scores(f)
                    if n:
                        add_output(n - 1)
                    if f < len(units):
                        rows32(f)
                    else:
                        norm_apply(dve, x, following, next_rstd_ready, next_xn_ready)
                    dve.wait_ge(o_mm, n + 1)
                    if c == 1:
                        dve.wait_ge(qs_ready, DREP * (g + 1))
                        dve.tensor_tensor(o_gated, bank4(banks[7]), scaled, ALU.add).then_inc(o_ready, 1)
                    else:
                        dve.tensor_copy(flat(o_gated), banks[7]).then_inc(o_ready, 1)
                    if f < len(units):
                        blocks64(f)
                    if n:
                        dve.wait_ge(rms_step, 2 * n)
                    dve.tensor_scalar(rms_a, sum_q[n % 2], L2_EPS, DK * LN_EPS, ALU.add, ALU.mult).then_inc(rms_step, 1)
                    dve.wait_ge(sum_o_ready, DREP * (n + 1))
                    dve.wait_ge(rms_step, 2 * n + 1)
                    if n:
                        dve.wait_ge(rms_ready, n)
                    dve.scalar_tensor_tensor(rms_b, sum_o, 1.0 / DK, rms_a, ALU.mult, ALU.add).then_inc(rms_step, 1)
                    if f < len(units):
                        rows64(f)
                    dve.wait_ge(rms_ready, n + 1)
                    dve.wait_ge(silu_g_ready, len(units))
                    for r in range(DREP):
                        dve.scalar_tensor_tensor(o_gated[:, r, :], o_gated[:, r, :], rms[:, r:r + 1], gate(n)[:, r * P:(r + 1) * P],
                                                 ALU.mult, ALU.mult).then_inc(gated_ready, 1)
                    if f < len(units):
                        block128(f)
                    if f == len(units) - 1:
                        dve.wait_ge(next_loaded, 16)
                        norm_stats(dve, x, following, next_stats, next_aggr, next_var_ready)
                    if n + 8 < len(step_tiles):
                        convolve(n + 8)
                add_output(len(units) - 1)
        nc.sync.sem_clear(C["all_sems"])
        nc.all_engine_barrier()


def lut_layer(nc, C, ar, banks, x, x_out):
    ar.at = 0
    w = norm_buffers(ar)
    gate = [ar.take(SEQ) for _ in range(2)]
    hT = [ar.take(SEQ) for _ in range(2)]

    with ExitStack() as st:
        sem = lambda n: st.enter_context(nc.semaphore(n))
        stats, aggr, var_ready = sem("stats"), sem("aggr"), sem("var_ready")
        rstd_ready, xn_ready, xnT_psum, xnT_ready = sem("rstd_ready"), sem("xn_ready"), sem("xnT_psum"), sem("xnT_ready")
        up_mm, gate_ready, hT_ready, down_mm, x_done, stored = (
            sem("up_mm"), sem("gate_ready"), sem("hT_ready"), sem("down_mm"), sem("x_done"), sem("stored"))
        with nc.Block() as block:
            @block.sync
            def _(sp):
                sp.wait_ge(x_done, NT)
                sp.dma_start(x_out, x[:, :, :]).then_inc(stored, 16)
                sp.wait_ge(stored, 16)

            @block.gpsimd
            def _(pool):
                norm_rstd(pool, C, w, var_ready, rstd_ready)

            @block.tensor
            def _(pe):
                norm_transpose(pe, C, w, banks[0], xn_ready, xnT_psum)
                pe.wait_ge(xnT_ready, 1)

                def up(n):
                    rows = min(P, FI - n * P)
                    if n >= 2:
                        pe.wait_ge(hT_ready, n - 1)
                    for half in range(2):
                        for k in range(KD):
                            mm = pe.matmul(banks[2 + n % 2][0:rows, half * SEQ:(half + 1) * SEQ],
                                           C["ffn_gu"][:, k, half, n * P:n * P + rows], w["xnT"][:, k, :],
                                           start=(k == 0), stop=(k == KD - 1))
                    mm.then_inc(up_mm, 1)

                def down(n):
                    rows = min(P, FI - n * P)
                    pe.wait_ge(hT_ready, n + 1)
                    for t in range(NT):
                        mm = pe.matmul(banks[4 + t][:, 0:D], hT[n % 2][0:rows, t * P:(t + 1) * P],
                                       C["ffn_down"][0:rows, n, :], start=(n == 0), stop=(n == FTILES - 1))
                    mm.then_inc(down_mm, 1)

                up(0)
                for n in range(FTILES):
                    if n + 1 < FTILES:
                        up(n + 1)
                    down(n)

            @block.scalar
            def _(act):
                norm_copy(act, w, banks[0], xnT_psum, xnT_ready)
                for n in range(FTILES):
                    rows = min(P, FI - n * P)
                    act.wait_ge(up_mm, n + 1)
                    if n >= 2:
                        act.wait_ge(hT_ready, n - 1)
                    act.activation(gate[n % 2][0:rows], banks[2 + n % 2][0:rows, 0:SEQ], ACT.Silu).then_inc(gate_ready, 1)

            @block.vector
            def _(dve):
                norm_stats(dve, x, w, stats, aggr, var_ready)
                norm_apply(dve, x, w, rstd_ready, xn_ready)
                for n in range(FTILES):
                    rows = min(P, FI - n * P)
                    dve.wait_ge(gate_ready, n + 1)
                    if n >= 2:
                        dve.wait_ge(down_mm, n - 1)
                    dve.tensor_tensor(hT[n % 2][0:rows], gate[n % 2][0:rows], banks[2 + n % 2][0:rows, SEQ:2 * SEQ],
                                      ALU.mult).then_inc(hT_ready, 1)
                dve.wait_ge(down_mm, FTILES)
                for t in range(NT):
                    dve.tensor_tensor(x[:, t, :], x[:, t, :], banks[4 + t][:, 0:D], ALU.add).then_inc(x_done, 1)
        nc.sync.sem_clear(C["all_sems"])
        nc.all_engine_barrier()


def build(nc, io, out):
    n_seq = io["x"].shape[0] - 1
    with ExitStack() as st:
        sb = lambda name, shape, dt=F32: st.enter_context(nc.sbuf_tensor(name, shape, dt))
        x = sb("x", [P, NT, D])
        x_prev = sb("x_prev", [P, NT, D])
        C = {"x_prev": x_prev[:, :, :]}
        loads, first_loads = [], []

        def weight(name, shape, src, loads=loads):
            t = sb(name, [P] + shape)
            C[name] = t[(slice(None),) * (1 + len(shape))]
            loads.append((C[name], src))

        halves = lambda ap: ap.rearrange("(k p) n -> p k n", p=P)
        weight("ident", [P], io["ident"], first_loads)
        weight("wqkv", [KD, NQKV], halves(io["wqkvT"]))
        weight("wo", [KD, D], halves(io["woT"]))
        weight("rope_cos", [NT, HD], io["rope_cos"].rearrange("(t p) n -> p t n", p=P))
        weight("rope_sin", [NT, HD], io["rope_sin"].rearrange("(t p) n -> p t n", p=P))
        weight("causal", [NSUB, SUB], io["causal"].rearrange("p (u k) -> p u k", k=SUB))
        weight("repeat_rows", [REP], io["repeat_rows"])
        weight("router", [KD, NE], halves(io["routerT"]))
        weight("earlier", [NE, NE], io["earlier"].rearrange("p (a b) -> p a b", b=NE))
        weight("gate_up", [KD, NE + 1, 2, INTER], io["gate_up"].rearrange("(k p) e h n -> p k e h n", p=P))
        weight("down", [NE + 1, D], io["down"].rearrange("e p n -> p e n"))
        weight("qkv_w", [KD, (DH + 2 * DKV) * DK], halves(io["qkv_wT"]))
        weight("conv_w", [DH + 2 * DKV, TAPS], io["conv_w"].rearrange("(c p) i -> p c i", p=P))
        weight("g_w", [KD, DH * DK], halves(io["g_wT"]))
        weight("bgk_w", [KD, 2 * DH], halves(io["bgk_wT"]))
        weight("o_w", [DH, D], io["o_wT"].rearrange("(h p) n -> p h n", p=P))
        weight("norm_w", [1], io["norm_w"].rearrange("(p a) -> p a", a=1))
        weight("lut", [LUT], io["lut"].rearrange("(a n) -> a n", a=1).broadcast_to([P, LUT]), first_loads)
        weight("incl", [P], io["incl"])
        weight("later", [P], io["later"])
        weight("cross64", [P], io["cross64"])
        weight("cross128", [P], io["cross128"])
        weight("before", [P], io["before"])
        C["ffn_gu"] = sb("ffn_gu", [P, KD, 2, FI])[:, :, :, :]
        C["ffn_down"] = sb("ffn_down", [P, FTILES, D])[:, :, :]
        C["v32"] = sb("v32", [P, NT, NKV, 32])[:, :, :, :]
        C["bd"] = sb("bd", [P, HEAD_TILES * REP * GROUPS * SEQ])[:, :]
        C["neg_half"] = sb("neg_half", [P, 8])[:, :]
        C["comb"] = sb("comb", [P, NT, NE + 1])[:, :, :]
        C["ones"] = sb("ones", [P, SUB])[:, :]
        size = WORK
        ar = Arena(sb("work", [P, size]), size)
        psum_scores = st.enter_context(nc.psum_tensor("psum_scores", [P, 3 * 512], F32))
        banks = [psum_scores[:, i * 512:(i + 1) * 512] for i in range(3)]
        banks += [st.enter_context(nc.psum_tensor(f"bank{i}", [P, 512], F32))[:, :] for i in range(3, 8)]
        C["psum_scores"] = psum_scores[:, :]
        chunks = []
        for half, name in enumerate(("gate_idxT", "up_idxT")):
            for k in range(KD):
                chunks.append((P, C["ffn_gu"][:, k, half, :], io[name][k * P:(k + 1) * P, :], FI, True))
        for i in range(FTILES):
            rows = min(P, FI - i * P)
            chunks.append((rows, C["ffn_down"][0:rows, i, :], io["down_idxT"][i * P:i * P + rows, :], D, i < FTILES - 1))
        C["ident_bf"] = sb("ident_bf", [P, P], BF16)[:, :]
        C["before_bf"] = sb("before_bf", [P, P], BF16)[:, :]
        scratch_dram = lambda name, shape: nc.dram_tensor(name, shape, F32, kind="Internal").ap()
        dram = {"bg": scratch_dram("scratch_bg", [2 * DH, SEQ]), "kk": scratch_dram("scratch_kk", [DKV, NSUB, SUB, SUB]),
                "u": scratch_dram("scratch_u", [DH * NSUB, SUB, SUB])}
        C["loads"], C["first_loads"], C["lut_chunks"] = loads, first_loads, chunks
        scratch = {"idx": [ar.take(FI).bitcast(I32) for _ in range(2)], "term": [ar.take(FI) for _ in range(4)]}
        with ExitStack() as s2:
            first = s2.enter_context(nc.semaphore("first")).num
        C["all_sems"] = range(first, 256)
        load_weights(nc, C, banks, scratch)
        first_projection(nc, C, ar, banks, x, io["x"][0].rearrange("(t p) n -> p t n", p=P))
        with nc.Fori(0, n_seq) as b:
            prev_out = out[bass.ds(b, 1)].rearrange("o (t p) n -> p (o t) n", p=P)
            next_in = io["x"][bass.ds(b + 1, 1)].rearrange("o (t p) n -> p (o t) n", p=P)
            attention_layer(nc, C, ar, banks, x)
            experts_layer(nc, C, ar, banks, x)
            delta_layer(nc, C, ar, banks, x, dram, x_prev, prev_out, next_in)
        lut_layer(nc, C, ar, banks, x_prev, out[n_seq].rearrange("(t p) n -> p t n", p=P))


def constants():
    i = np.arange(P)
    inv_freq = (1.0 / np.float32(10000.0) ** (np.arange(0, HD, 2, dtype=np.float32) / np.float32(HD))).astype(np.float32)
    freqs = np.outer(np.arange(SEQ, dtype=np.float32), inv_freq).astype(np.float32)
    cos, sin = np.cos(freqs), np.sin(freqs)
    cos = np.stack([cos, cos], -1).reshape(SEQ, HD)
    sin = np.stack([-sin, sin], -1).reshape(SEQ, HD)
    sub = i // SUB
    return {
        "ident": np.eye(P, dtype=np.float32),
        "rope_cos": cos.astype(np.float32),
        "rope_sin": sin.astype(np.float32),
        "causal": np.concatenate([np.zeros((P, P)), np.where(i[None, :] > i[:, None], BIG, 0.0)], 1).astype(np.float32),
        "repeat_rows": (i[:, None] % 32 // HD == np.arange(REP)[None, :]).astype(np.float32) * np.float32(-(HD ** -0.5)),
        "earlier": np.tile((np.arange(NE)[None, :] < np.arange(NE)[:, None]).reshape(1, -1), (P, 1)).astype(np.float32),
        "incl": (i[:, None] <= i[None, :]).astype(np.float32),
        "later": (i[:, None] > i[None, :]).astype(np.float32),
        "cross64": ((sub[:, None] // 2 == sub[None, :] // 2) & (sub[:, None] > sub[None, :])).astype(np.float32),
        "cross128": ((i[:, None] >= 64) & (i[None, :] < 64)).astype(np.float32),
        "before": np.where(i[:, None] > i[None, :], -BEFORE, 0.0).astype(np.float32),
    }


def host_layout(inp):
    a = {k: np.asarray(v) for k, v in inp.items()}
    T = lambda m: np.ascontiguousarray(m.T)
    gate = np.concatenate([a["L0_ffn_Wg"], a["L0_ffn_Wg_s"][None]], 0)
    up = np.concatenate([a["L0_ffn_Wu"], a["L0_ffn_Wu_s"][None]], 0)
    return {
        "x": np.concatenate([a["L0_attn_x"], a["L0_attn_x"][:1]], 0),
        "wqkvT": T(np.concatenate([a["L0_attn_wq"], a["L0_attn_wk"], a["L0_attn_wv"]], 0)),
        "woT": T(a["L0_attn_wo"]),
        "routerT": T(a["L0_ffn_Wr"]),
        "gate_up": np.ascontiguousarray(np.stack([gate, up], 0).transpose(2, 1, 0, 3)),
        "down": np.concatenate([a["L0_ffn_Wd"], a["L0_ffn_Wd_s"][None]], 0),
        "qkv_wT": T(a["L1_attn_qkv_w"]),
        "conv_w": a["L1_attn_conv_w"],
        "g_wT": T(a["L1_attn_g_w"]),
        "bgk_wT": T(np.concatenate([a["L1_attn_b_w"], a["L1_attn_gk_w"]], 0)),
        "o_wT": T(a["L1_attn_o_w"]),
        "norm_w": a["L1_attn_out_norm_w"],
        "lut": a["L1_ffn_lut"],
        "gate_idxT": T(a["L1_ffn_gate_idx"]),
        "up_idxT": T(a["L1_ffn_up_idx"]),
        "down_idxT": T(a["L1_ffn_down_idx"]),
    }


def kernel(**inputs):
    import concourse.bacc as bacc
    from concourse.bass_utils import run_bass_kernel_spmd

    arrays = host_layout(inputs)
    arrays.update(constants())
    n_seq = arrays["x"].shape[0] - 1
    nc = bacc.Bacc("TRN2", target_bir_lowering=False, num_devices=1)
    io = {n: nc.dram_tensor(f"in_{n}", a.shape, mybir.dt.from_np(a.dtype), kind="ExternalInput").ap()
          for n, a in arrays.items()}
    out = nc.dram_tensor("out", (n_seq + 1, SEQ, D), F32, kind="ExternalOutput").ap()
    build(nc, io, out)
    result = run_bass_kernel_spmd(nc, [{f"in_{n}": a for n, a in arrays.items()}], core_ids=[0])
    return result.results[0]["out"][1:]
```
